# Optimizing a Trainium2 kernel written in Bass

```python
import numpy as np
import jax
import jax.numpy as jnp

def _softmax(x, axis=-1):
    return jax.nn.softmax(x, axis=axis)

def _gelu(x):
    return jax.nn.gelu(x, approximate=True)

def _silu(x):
    return jax.nn.silu(x)

def _sigmoid(x):
    return jax.nn.sigmoid(x)

def _layernorm(x, axis=-1, eps=1e-05):
    m = jnp.mean(x, axis=axis, keepdims=True)
    v = jnp.var(x, axis=axis, keepdims=True)
    return (x - m) / jnp.sqrt(v + eps)

def _scatter_add(tgt, idx, src, axis=0):
    return tgt.at[idx].add(src)

def _segment_sum(src, seg, n):
    return jax.ops.segment_sum(src, seg, n)
kernel_name = 'mk_adaln_d1_jaxref_r8_e23f24'

def setup_inputs(seed: int=0):
    np.random.seed(seed)
    _w = jnp.asarray

    def _L0_attn_setup():
        import jax, jax.numpy as jnp
        import numpy as np
        HIDDEN = 128
        B, S = (8, 256)
        key = jax.random.key(seed)
        k_in, k_w, k_b = jax.random.split(key, 3)
        inputs = jax.random.normal(k_in, (B, S, HIDDEN), dtype=jnp.float32)
        Wq = jax.random.normal(k_w, (HIDDEN, HIDDEN), dtype=jnp.float32) / np.sqrt(HIDDEN)
        bq = jax.random.normal(k_b, (HIDDEN,), dtype=jnp.float32) * 0.01
        return {'inputs': inputs, 'Wq': Wq, 'bq': bq}
    _L0_attn_in = _L0_attn_setup()

    def _L0_ffn_setup():
        import jax, jax.numpy as jnp
        import numpy as np
        B, S, H, FFN, E = (2, 256, 128, 512, 8)
        key = jax.random.key(seed)
        k0, k1, k2, k3 = jax.random.split(key, 4)
        return {'hidden_states': jax.random.normal(k0, (B, S, H), dtype=jnp.float32), 'Wr': jax.random.normal(k1, (H, E), dtype=jnp.float32) * 0.02, 'br': jnp.zeros((E,), dtype=jnp.float32), 'W1': jax.random.normal(k2, (E, H, FFN), dtype=jnp.float32) * 0.02, 'W2': jax.random.normal(k3, (E, FFN, H), dtype=jnp.float32) * 0.02}
    _L0_ffn_in = _L0_ffn_setup()
    _L0_c = _w((lambda *s: np.random.randn(*s).astype(np.float32) * 0.05)(16, 128))
    _L0_wmod = _w((lambda *s: np.random.randn(*s).astype(np.float32) * 0.05)(128, 6 * 128) * 128 ** (-0.5))
    _d = {'L0_attn_inputs': _L0_attn_in['inputs'], 'L0_attn_Wq': _L0_attn_in['Wq'], 'L0_attn_bq': _L0_attn_in['bq'], 'L0_ffn_Wr': _L0_ffn_in['Wr'], 'L0_ffn_br': _L0_ffn_in['br'], 'L0_ffn_W1': _L0_ffn_in['W1'], 'L0_ffn_W2': _L0_ffn_in['W2'], 'L0_c': _L0_c, 'L0_wmod': _L0_wmod}
    _x0 = _d['L0_attn_inputs']
    _d['L0_attn_inputs'] = jax.random.normal(jax.random.fold_in(jax.random.key(seed), 1), (16, 512, 128), dtype=_x0.dtype)
    del _x0
    return _d

def reference(L0_attn_inputs, L0_attn_Wq, L0_attn_bq, L0_ffn_Wr, L0_ffn_br, L0_ffn_W1, L0_ffn_W2, L0_c, L0_wmod):

    def _L0_attn_ref(inputs, Wq, bq):
        import jax, jax.numpy as jnp
        import numpy as np
        HIDDEN = 128
        B, S = (8, 256)
        Q = jnp.einsum('bsh,hd->bsd', inputs, Wq) + bq
        K = Q
        V = Q
        scale = 1.0 / jnp.sqrt(jnp.float32(HIDDEN))
        scores = jnp.einsum('bqh,bkh->bqk', Q, K) * scale
        probs = jax.nn.softmax(scores, axis=-1)
        out = jnp.einsum('bqk,bkh->bqh', probs, V)
        return out

    def _L0_ffn_ref(hidden_states, Wr, br, W1, W2):
        import jax, jax.numpy as jnp
        import numpy as np
        B, S, H, FFN, E = (2, 256, 128, 512, 8)
        b, s, h = hidden_states.shape
        x = hidden_states.reshape(-1, h)
        route = jax.nn.sigmoid(x @ Wr + br)
        max_prob = jnp.max(route, axis=1, keepdims=True)
        max_ind = jnp.argmax(route, axis=1)
        out = jnp.zeros_like(x)
        n_experts = Wr.shape[1]
        for e in range(n_experts):
            mask = (max_ind == e)[:, None].astype(x.dtype)
            y = jax.nn.gelu(x @ W1[e], approximate=False) @ W2[e]
            out = out + mask * y
        out = out * max_prob
        return out.reshape(b, s, h)
    x = L0_attn_inputs
    mod = (_silu(L0_c) @ L0_wmod).reshape(L0_c.shape[0], 6, 1, -1)
    sa, ca, ga, sb, cb, gb = (mod[:, 0], mod[:, 1], mod[:, 2], mod[:, 3], mod[:, 4], mod[:, 5])
    ga = (2 * (ga >= 0) - 1) * jnp.maximum(jnp.abs(ga), 0.25)
    gb = (2 * (gb >= 0) - 1) * jnp.maximum(jnp.abs(gb), 0.25)
    h = _layernorm(x, axis=-1) * (1 + ca) + sa
    x = x + ga * _L0_attn_ref(h, L0_attn_Wq, L0_attn_bq)
    h = _layernorm(x, axis=-1) * (1 + cb) + sb
    x = x + gb * _L0_ffn_ref(h, L0_ffn_Wr, L0_ffn_br, L0_ffn_W1, L0_ffn_W2)
    return x

_drawn_inputs = setup_inputs


def setup_inputs(seed=0):
    import zlib

    import numpy as np

    out = dict(_drawn_inputs(seed))
    spreads = {'L0_ffn_br': (0.0, 0.8)}
    factors = {'L0_attn_bq': 8.0, 'L0_ffn_Wr': 8.0, 'L0_ffn_W1': 7.475, 'L0_ffn_W2': 7.415}
    for name, (base, spread) in spreads.items():
        noise = np.random.default_rng([zlib.crc32(name.encode()), seed]).standard_normal(out[name].shape)
        drawn = base * np.exp(spread * noise) if base else spread * noise
        out[name] = jnp.asarray(drawn.astype(out[name].dtype))
    for name, factor in factors.items():
        out[name] = (out[name] * factor).astype(out[name].dtype)
    return out
```

```python
from collections import namedtuple
from contextlib import ExitStack

import concourse.bass as bass
from concourse import mybir

P = 128
F32 = mybir.dt.float32
F32R = mybir.dt.float32r
BF16 = mybir.dt.bfloat16
I32 = mybir.dt.int32
ALU = mybir.AluOpType
ACT = mybir.ActivationFunctionType
AX_X = mybir.AxisListType.X
EPS = 1e-5

Batch = namedtuple("Batch", "n p h")


def batch_at(i, k):
    return Batch(2 * i + k, k % 2, i + k // 2)


def adaln_block(nc, x_in, Wq, bq, Wr, br, W1, W2, c_in, wmod, out):
    B, S, H = x_in.shape
    E, _, F = W1.shape
    J = S // P
    KF = F // P
    N = B * S
    SCALE = float(H) ** -0.5
    ROW = 3 * H + 4
    ROW_X1, ROW_GATE, ROW_ID = H, 2 * H, 3 * H
    REGION = N + P
    TILES = N // P + E - 1
    RING = 6
    assert H == P and J == 4 and F == 512

    rows_dram = nc.dram_tensor("sorted_rows", [E * REGION + P, ROW], F32).ap()
    mod_dram = nc.dram_tensor("modulation_rows", [B, 4 * H], F32).ap()
    x_view = x_in.rearrange("b (p j) h -> b p (j h)", j=J)
    out_rows = out.rearrange("b s h -> (b s) h")

    with ExitStack() as ctx:
        def sb(name, shape, dt=F32):
            return ctx.enter_context(nc.sbuf_tensor(name, shape, dt))

        def sem(name):
            return ctx.enter_context(nc.semaphore(name))

        scores = [ctx.enter_context(nc.psum_tensor(f"scores{n}", [P, 512], F32)) for n in range(2)]
        flipped = [ctx.enter_context(nc.psum_tensor(f"flipped{n}", [P, 512], F32)) for n in range(2)]
        mixed = [ctx.enter_context(nc.psum_tensor(f"mixed{n}", [P, 512], F32)) for n in range(2)]
        side = [ctx.enter_context(nc.psum_tensor(f"side{n}", [P, 512], F32)) for n in range(2)]

        ident = sb("ident", [P, P])
        upper = sb("upper", [P, P], BF16)
        ones = sb("ones", [P, P], BF16)
        neg_half = sb("neg_half", [P, J])
        region_i = sb("region_i", [P, E + 1], I32)
        region = sb("region", [P, E + 1])
        order_i = sb("order_i", [P, E], I32)
        order = sb("order", [P, E])
        token_id = sb("token_id", [P, B * J], I32)
        tile_i = sb("tile_i", [1, TILES], I32)
        tile_no = sb("tile_no", [1, TILES])
        pad_rows = sb("pad_rows", [P, ROW])

        wq_sb = sb("wq_sb", [P, H])
        bq_sb = sb("bq_sb", [P, 1])
        wr_sb = sb("wr_sb", [P, E])
        br_sb = sb("br_sb", [P, E])
        w1_raw = sb("w1_raw", [P, 2, F])
        w1_hi = sb("w1_hi", [P, E * F], F32R)
        w1_lo = sb("w1_lo", [P, E * F], F32R)
        w2_sb = sb("w2_sb", [P, E * F])
        cond = sb("cond", [B, H])
        cond_e = sb("cond_e", [B, H])
        cond_d = sb("cond_d", [B, H])
        cond_s = sb("cond_s", [B, H])
        silu = sb("silu", [B, H])
        silu_t = sb("silu_t", [P, B])
        wmod_sb = sb("wmod_sb", [P, 6 * H])
        shift1 = sb("shift1", [P, B])
        scale1 = sb("scale1", [P, B])
        shift2 = sb("shift2", [P, B])
        scale2 = sb("scale2", [P, B])
        mod_rows = sb("mod_rows", [B, 4 * H])
        gate_sign = sb("gate_sign", [B, 2 * H])
        gate_neg = sb("gate_neg", [B, 2 * H])
        gate_size = sb("gate_size", [B, 2 * H])
        mod_all = sb("mod_all", [P, B, 4 * H])

        x_all = sb("x_all", [P, B, J * H])
        stats1 = sb("stats1", [P, 2, J, 6])
        stats2 = sb("stats2", [P, 2, J, 6])
        moments1 = sb("moments1", [P, 2, J, 2])
        moments2 = sb("moments2", [P, 2, J, 2])
        var1 = sb("var1", [P, 2, J])
        var2 = sb("var2", [P, 2, J])
        rstd1 = sb("rstd1", [P, 2, J])
        rstd2 = sb("rstd2", [P, 2, J])
        xn = sb("xn", [P, J, H])
        h_t = sb("h_t", [P, J * P])
        q_t = sb("q_t", [P, 2, J * P])
        q_hi = sb("q_hi", [P, 2, J * P], F32R)
        q_lo = sb("q_lo", [P, 2, J * P], F32R)
        v_sb = sb("v_sb", [P, 2, J, H])
        row_max = sb("row_max", [P, 2 * J])
        neg_max = sb("neg_max", [P, 2 * J])
        den = sb("den", [P, 2 * J])
        den_inv = sb("den_inv", [P, 2 * J])
        probs = sb("probs", [P, 2, 512])
        probs_t = sb("probs_t", [P, 2, 512])
        xn2 = sb("xn2", [P, J, H])
        h2_t = sb("h2_t", [P, J * P])
        payload = sb("payload", [P, 2, J, ROW])
        logit = sb("logit", [P, J * E])
        logit_e = sb("logit_e", [P, J * E])
        logit_d = sb("logit_d", [P, J * E])
        route = sb("route", [P, J, E])
        route_max = sb("route_max", [P, 2, J])
        at_max = sb("at_max", [P, J, E])
        ranked = sb("ranked", [P, J, E])
        rank_max = sb("rank_max", [P, J])
        mask = sb("mask", [P, J, E], BF16)
        place = sb("place", [P, J, E])
        placed = sb("placed", [P, J, E])
        slots = sb("slots", [P, 2 * J], I32)
        batch_count = sb("batch_count", [P, E])
        seen = sb("seen", [P, E], BF16)

        counts = sb("counts", [P, E])
        padded_i = sb("padded_i", [P, E], I32)
        tiles_i = sb("tiles_i", [P, E], I32)
        n_tiles = sb("n_tiles", [P, E])
        one_row = sb("one_row", [P, E])
        tiles_to = sb("tiles_to", [P, E + 1])
        base = sb("base", [P, E + 1])
        base_step = sb("base_step", [P, E])
        passed = sb("passed", [1, TILES, E])
        steps = sb("steps", [1, TILES, E])
        owner = sb("owner", [1, TILES])
        start = sb("start", [1, TILES])
        start_f = sb("start_f", [1, TILES])
        tile_weights = sb("tile_weights", [1, TILES], I32)
        tile_row = sb("tile_row", [1, TILES], I32)
        tail_row = sb("tail_row", [1, E], I32)

        rows = sb("rows", [P, RING, ROW])
        f_hi = sb("f_hi", [P, 2, P], F32R)
        f_lo = sb("f_lo", [P, 2, P], F32R)
        gated = sb("gated", [P, 2, H])
        y_out = sb("y_out", [P, RING, H])

        s_consts = sem("s_consts")
        s_pool = sem("s_pool")
        s_small = sem("s_small")
        s_small2 = sem("s_small2")
        s_dve0 = sem("s_dve0")
        s_cond_e = sem("s_cond_e")
        s_silu = sem("s_silu")
        s_silu_tp = sem("s_silu_tp")
        s_silu_t = sem("s_silu_t")
        s_cols = sem("s_cols")
        s_rowsp = sem("s_rowsp")
        s_mod = sem("s_mod")
        s_mod_dram = sem("s_mod_dram")
        s_pad0 = sem("s_pad0")
        x_loaded = [sem(f"x_loaded{n}") for n in range(2)]
        mod_loaded = [sem(f"mod_loaded{n}") for n in range(2)]
        w1_loaded = [sem(f"w1_loaded{n}") for n in range(2)]
        w2_loaded = sem("w2_loaded")
        w1_split = sem("w1_split")
        w1_half = sem("w1_half")
        ln1_stats = sem("ln1_stats")
        ln1_moments = sem("ln1_moments")
        var1_ready = sem("var1_ready")
        rstd1_ready = sem("rstd1_ready")
        xn_ready = sem("xn_ready")
        xn_flipped = sem("xn_flipped")
        h_ready = sem("h_ready")
        q_projected = sem("q_projected")
        q_ready = sem("q_ready")
        q_hi_ready = sem("q_hi_ready")
        q_split = sem("q_split")
        v_flipped = sem("v_flipped")
        v_ready = sem("v_ready")
        scores_ready = sem("scores_ready")
        max_found = sem("max_found")
        max_ready = sem("max_ready")
        exp_done = sem("exp_done")
        probs_flipped = sem("probs_flipped")
        probs_t_ready = sem("probs_t_ready")
        attn_done = sem("attn_done")
        den_ready = sem("den_ready")
        x1_ready = sem("x1_ready")
        ln2_stats = sem("ln2_stats")
        ln2_moments = sem("ln2_moments")
        var2_ready = sem("var2_ready")
        rstd2_ready = sem("rstd2_ready")
        xn2_ready = sem("xn2_ready")
        xn2_flipped = sem("xn2_flipped")
        h2t_ready = sem("h2t_ready")
        logits_ready = sem("logits_ready")
        logit_ready = sem("logit_ready")
        logit_e_ready = sem("logit_e_ready")
        route_link = sem("route_link")
        mask_ready = sem("mask_ready")
        places_ready = sem("places_ready")
        place_link = sem("place_link")
        slots_ready = sem("slots_ready")
        seen_ready = sem("seen_ready")
        x1_copied = sem("x1_copied")
        gates_ready = sem("gates_ready")
        h2_scaled = sem("h2_scaled")
        h2_ready = sem("h2_ready")
        scattered = [sem(f"scattered{n}") for n in range(2)]
        counts_ready = sem("counts_ready")
        plan_link = sem("plan_link")
        plan_ready = sem("plan_ready")
        tails_ready = sem("tails_ready")
        tails_filled = sem("tails_filled")
        rows_loaded = [sem(f"rows_loaded{n}") for n in range(RING)]
        f_flipped = sem("f_flipped")
        f_hi_ready = sem("f_hi_ready")
        f_split = sem("f_split")
        up_done = sem("up_done")
        gelu_done = sem("gelu_done")
        gelu_flipped = sem("gelu_flipped")
        gelu_t_ready = sem("gelu_t_ready")
        down_done = sem("down_done")
        gated_ready = sem("gated_ready")
        y_ready = sem("y_ready")
        y_scattered = [sem(f"y_scattered{n}") for n in range(RING)]

        def wait(eng, s, value):
            if not isinstance(value, int) or value > 0:
                eng.wait_ge(s, value)

        def wait_apart(eng, s, value):
            if not isinstance(value, int):
                value = eng.to_reg(value)
                eng.wait_ge(x_loaded[0], 16)
            wait(eng, s, value)

        def real(b):
            return not isinstance(b.n, int) or 0 <= b.n < B

        LOOP_FROM, LOOP_TO = 1, B // 2 - 1

        def attention_slots(eng, slot):
            for k in range(-2, 2 * LOOP_FROM):
                slot(0, k)
            with eng.Fori(LOOP_FROM, LOOP_TO) as i:
                for k in range(2):
                    slot(i, k)
            for k in range(2 * LOOP_TO, B + 2):
                slot(0, k)

        FFN_FROM, FFN_TO = 1, (TILES - 2) // RING

        def ffn_slots(eng, slot):
            for k in range(-2, RING * FFN_FROM):
                slot(0, k)
            with eng.Fori(FFN_FROM, FFN_TO) as i:
                for k in range(RING):
                    slot(i, k)
            for k in range(RING * FFN_TO, TILES + 1):
                slot(0, k)

        def real_tile(t):
            return not isinstance(t, int) or 0 <= t < TILES

        block = ctx.enter_context(nc.Block())

        @block.sync
        def _(sp):
            sp.dma_start(cond[:], c_in).then_inc(s_small, 16)
            sp.dma_start(x_all[:, 0, :], x_view[0]).then_inc(x_loaded[0], 16)
            sp.dma_start(wmod_sb[:], wmod).then_inc(s_small2, 16)
            sp.dma_start(x_all[:, 1, :], x_view[1]).then_inc(x_loaded[1], 16)
            sp.wait_ge(s_mod, 1)
            sp.dma_start(mod_dram, mod_rows[:]).then_inc(s_mod_dram, 16)
            sp.wait_ge(s_mod_dram, 16)
            for n in range(2):
                sp.dma_start(mod_all[:, n, :], mod_dram[n:n + 1, :].partition_broadcast(P)
                             if False else mod_dram[n:n + 1, :].to_broadcast([P, 4 * H])
                             ).then_inc(mod_loaded[n], 16)
            with sp.Fori(1, B // 2) as i:
                for n in range(2):
                    sp.wait_ge(x_loaded[n], 16 * i)
                    sp.dma_start(x_all[:, bass.ds(2 * i + n, 1), :],
                                 x_view[bass.ds(2 * i + n, 1)].rearrange("b p f -> p b f")
                                 ).then_inc(x_loaded[n], 16)
                    wait_apart(sp, mod_loaded[n], 16 * i)
                    sp.dma_start(mod_all[:, bass.ds(2 * i + n, 1), :],
                                 mod_dram[bass.ds(2 * i + n, 1), :].unsqueeze(0).to_broadcast([P, 1, 4 * H])
                                 ).then_inc(mod_loaded[n], 16)
            sp.wait_ge(s_pad0, 2)
            sp.dma_start(rows_dram[E * REGION:, :], pad_rows[:]).then_inc(tails_filled, 16)
            sp.wait_ge(tails_ready, 1)
            for e in range(E):
                first = sp.value_load(tail_row[0:1, e:e + 1], min_val=0, max_val=(E - 1) * REGION + N)
                sp.dma_start(rows_dram[bass.ds(first, P), :], pad_rows[:]).then_inc(tails_filled, 16)
            for n in range(2):
                sp.wait_ge(scattered[n], 16 * J * (B // 2))
            sp.wait_ge(tails_filled, 16 * (E + 1))
            sp.wait_ge(plan_ready, 1)

            def load(i, k):
                t = RING * i + k
                wait(sp, y_scattered[k % RING], 16 * (i + k // RING))
                at = bass.ds(t, 1) if not isinstance(t, int) else slice(t, t + 1)
                first = sp.value_load(tile_row[0:1, at], min_val=0, max_val=E * REGION)
                sp.dma_start(rows[:, k % RING, :], rows_dram[bass.ds(first, P), :]
                             ).then_inc(rows_loaded[k % RING], 16)

            for k in range(RING):
                load(0, k)
            with sp.Fori(1, TILES // RING) as i:
                for k in range(RING):
                    load(i, k)
            for k in range(RING * (TILES // RING), TILES):
                load(0, k)
            for k in range(RING):
                sp.wait_ge(y_scattered[k], 16 * ((TILES - k + RING - 1) // RING))

        @block.tensor
        def _(pe):
            pe.wait_ge(s_silu, 1)
            pe.wait_ge(s_consts, 1)
            nc.tensor.transpose(side[0][:, 0:B], silu[:], ident[0:B, 0:B]).then_inc(s_silu_tp, 1)
            pe.wait_ge(s_silu_t, 1)
            pe.wait_ge(s_small2, 16)
            for n, part in enumerate((0, 1, 3, 4)):
                last = nc.tensor.matmul(side[1][:, n * B:(n + 1) * B], wmod_sb[:, part * H:(part + 1) * H],
                                        silu_t[:], start=True, stop=True)
            last.then_inc(s_cols, 1)
            for n, part in enumerate((2, 4, 3, 5)):
                last = nc.tensor.matmul(mixed[1][0:B, n * H:(n + 1) * H], silu_t[:],
                                        wmod_sb[:, part * H:(part + 1) * H], start=True, stop=True)
            last.then_inc(s_rowsp, 1)

            def flip_xn(b):
                if not real(b):
                    return
                pe.wait_ge(xn_ready, b.n + 1)
                if isinstance(b.n, int) and b.n == 0:
                    pe.wait_ge(s_dve0, 6)
                wait(pe, v_ready, b.n)
                for j in range(J):
                    last = nc.tensor.transpose(side[1][:, j * P:(j + 1) * P], xn[:, j, :], ident[:])
                last.then_inc(xn_flipped, 1)

            def project(b):
                if not real(b):
                    return
                pe.wait_ge(h_ready, b.n + 1)
                if isinstance(b.n, int) and b.n == 0:
                    pe.wait_ge(s_small, 80)
                nc.tensor.matmul(side[1][:], wq_sb[:], h_t[:], start=True, stop=True).then_inc(q_projected, 1)

            def flip_v(b):
                if not real(b):
                    return
                pe.wait_ge(q_ready, b.n + 1)
                for j in range(J):
                    last = nc.tensor.transpose(side[1][:, j * P:(j + 1) * P],
                                               q_t[:, b.p, j * P:(j + 1) * P], ident[:])
                last.then_inc(v_flipped, 1)

            def score(b, j):
                if not real(b):
                    return
                if j == 0:
                    pe.wait_ge(q_split, b.n + 1)
                wait(pe, exp_done, J * b.n + j - 1)
                mine = slice(j * P, (j + 1) * P)
                o = scores[j % 2][:]
                nc.tensor.matmul(o, q_lo[:, b.p, mine], q_hi[:, b.p, :], start=True, stop=False)
                nc.tensor.matmul(o, q_hi[:, b.p, mine], q_lo[:, b.p, :], start=False, stop=False)
                nc.tensor.matmul(o, q_hi[:, b.p, mine], q_hi[:, b.p, :], start=False, stop=True
                                 ).then_inc(scores_ready, 1)

            def flip_probs(b, j):
                if not real(b):
                    return
                pe.wait_ge(exp_done, J * b.n + j + 1)
                wait(pe, probs_t_ready, J * b.n + j - 1)
                for k in range(J):
                    last = nc.tensor.transpose(flipped[j % 2][:, k * P:(k + 1) * P],
                                               probs[:, j % 2, k * P:(k + 1) * P], ident[:])
                last.then_inc(probs_flipped, 1)

            def mix(b, j):
                if not real(b):
                    return
                pe.wait_ge(probs_t_ready, J * b.n + j + 1)
                if j == 0:
                    pe.wait_ge(v_ready, b.n + 1)
                wait(pe, x1_ready, J * b.n + j - 1)
                for k in range(J):
                    last = nc.tensor.matmul(mixed[j % 2][:, 0:H], probs_t[:, j % 2, k * P:(k + 1) * P],
                                            v_sb[:, b.p, k, :], start=(k == 0), stop=(k == J - 1))
                last.then_inc(attn_done, 1)

            def flip_xn2(b):
                if not real(b):
                    return
                pe.wait_ge(xn2_ready, b.n + 1)
                wait(pe, slots_ready, b.n)
                for j in range(J):
                    last = nc.tensor.transpose(side[0][:, j * P:(j + 1) * P], xn2[:, j, :], ident[:])
                last.then_inc(xn2_flipped, 1)

            def router(b):
                if not real(b):
                    return
                pe.wait_ge(h2t_ready, b.n + 1)
                for j in range(J):
                    last = nc.tensor.matmul(side[0][:, j * E:(j + 1) * E], h2_t[:, j * P:(j + 1) * P],
                                            wr_sb[:], start=True, stop=True)
                last.then_inc(logits_ready, 1)

            def places(b):
                if not real(b):
                    return
                pe.wait_ge(mask_ready, b.n + 1)
                pe.wait_ge(seen_ready, b.n + 1)
                o = side[0][:, 0:J * E].rearrange("p (j e) -> p j e", e=E)
                nc.tensor.matmul(o, upper[:], mask[:], start=True, stop=False)
                nc.tensor.matmul(o, ones[:], seen[:].unsqueeze(1).to_broadcast([P, J, E]),
                                 start=False, stop=False)
                for d in range(1, J):
                    last = nc.tensor.matmul(o[:, d:J, :], ones[:], mask[:, 0:J - d, :],
                                            start=False, stop=(d == J - 1))
                last.then_inc(places_ready, 1)

            def slot(i, k):
                now, after, prev = batch_at(i, k), batch_at(i, k + 1), batch_at(i, k - 1)
                score(now, 1)
                flip_probs(now, 0)
                mix(prev, 3)
                project(after)
                score(now, 2)
                flip_probs(now, 1)
                mix(now, 0)
                flip_v(after)
                score(now, 3)
                flip_xn2(prev)
                flip_probs(now, 2)
                mix(now, 1)
                flip_xn(batch_at(i, k + 2))
                score(after, 0)
                router(prev)
                flip_probs(now, 3)
                mix(now, 2)
                places(prev)

            attention_slots(pe, slot)
            pe.wait_ge(seen_ready, B + 1)
            nc.tensor.matmul(side[1][:, 0:E], ones[:], seen[:], start=True, stop=True).then_inc(counts_ready, 1)

            def weights_of(t):
                at = bass.ds(t, 1) if not isinstance(t, int) else slice(t, t + 1)
                return pe.value_load(tile_weights[0:1, at], min_val=0, max_val=(E - 1) * F)

            def flip_rows(i, k):
                t = RING * i + k
                if not real_tile(t):
                    return
                pe.wait_ge(rows_loaded[k % RING], 16 * (i + k // RING + 1))
                wait(pe, f_split, t - 1)
                nc.tensor.transpose(side[k % 2][:, 0:P], rows[:, k % RING, 0:H], ident[:]).then_inc(f_flipped, 1)

            def up(i, k):
                t = RING * i + k
                if not real_tile(t):
                    return
                w = weights_of(t)
                pe.wait_ge(f_split, t + 1)
                wait(pe, gelu_done, t - 1)
                o = scores[k % 2][:]
                nc.tensor.matmul(o, f_lo[:, k % 2, :], w1_hi[:, bass.ds(w, F)], start=True, stop=False)
                nc.tensor.matmul(o, f_hi[:, k % 2, :], w1_lo[:, bass.ds(w, F)], start=False, stop=False)
                nc.tensor.matmul(o, f_hi[:, k % 2, :], w1_hi[:, bass.ds(w, F)], start=False, stop=True
                                 ).then_inc(up_done, 1)

            def flip_gelu(i, k):
                t = RING * i + k
                if not real_tile(t):
                    return
                pe.wait_ge(gelu_done, t + 1)
                wait(pe, gelu_t_ready, t - 1)
                for f in range(KF):
                    last = nc.tensor.transpose(flipped[k % 2][:, f * P:(f + 1) * P],
                                               probs[:, k % 2, f * P:(f + 1) * P], ident[:])
                last.then_inc(gelu_flipped, 1)

            def down(i, k):
                t = RING * i + k
                if not real_tile(t):
                    return
                w = weights_of(t)
                pe.wait_ge(gelu_t_ready, t + 1)
                wait(pe, gated_ready, t - 1)
                for f in range(KF):
                    last = nc.tensor.matmul(mixed[k % 2][:, 0:H], probs_t[:, k % 2, f * P:(f + 1) * P],
                                            w2_sb[:, bass.ds(w + f * H, H)],
                                            start=(f == 0), stop=(f == KF - 1))
                last.then_inc(down_done, 1)

            def ffn_slot(i, k):
                flip_rows(i, k + 2)
                up(i, k + 1)
                flip_gelu(i, k)
                down(i, k - 1)

            pe.wait_ge(plan_ready, 1)
            pe.wait_ge(w1_split, E)
            pe.wait_ge(w2_loaded, 16)
            ffn_slots(pe, ffn_slot)

        @block.scalar
        def _(act):
            act.dma_start(wq_sb[:], Wq).then_inc(s_small, 16)
            act.dma_start(bq_sb[:], bq.rearrange("(p a) -> p a", a=1)).then_inc(s_small, 16)
            act.dma_start(wr_sb[:], Wr).then_inc(s_small, 16)
            act.dma_start(br_sb[:], br.rearrange("(a e) -> a e", a=1).to_broadcast([P, E])).then_inc(s_small, 16)
            act.wait_ge(s_small, 80)
            nc.scalar.activation(cond_e[:], cond[:], ACT.Exp, scale=-1.0).then_inc(s_cond_e, 1)

            def load_w1(e):
                wait(act, w1_split, e - 1)
                act.dma_start(w1_raw[:, e % 2, :], W1[e]).then_inc(w1_loaded[e % 2], 16)

            def input_t(b):
                if not real(b):
                    return
                act.wait_ge(xn_flipped, b.n + 1)
                if isinstance(b.n, int) and b.n == 0:
                    act.wait_ge(s_dve0, 6)
                wait(act, q_projected, b.n)
                col = slice(b.n, b.n + 1) if isinstance(b.n, int) else bass.ds(b.n, 1)
                nc.scalar.activation(h_t[:], side[1][:], ACT.Identity, bias=shift1[:, col],
                                     scale=scale1[:, col]).then_inc(h_ready, 1)

            def query(b):
                if not real(b):
                    return
                act.wait_ge(q_projected, b.n + 1)
                wait(act, q_split, b.n - 1)
                wait(act, v_ready, b.n - 1)
                nc.scalar.activation(q_t[:, b.p, :], side[1][:], ACT.Identity, bias=bq_sb[:, 0:1]
                                     ).then_inc(q_ready, 1)

            def exps(b, j):
                if not real(b):
                    return
                act.wait_ge(max_ready, J * b.n + j + 1)
                wait(act, probs_flipped, J * b.n + j - 1)
                wait(act, x1_ready, J * (b.n - 2) + j + 1)
                c = b.p * J + j
                nc.scalar.activation(probs[:, j % 2, :], scores[j % 2][:], ACT.Exp, bias=neg_max[:, c:c + 1],
                                     scale=SCALE, accum_out=den[:, c:c + 1]).then_inc(exp_done, 1)

            def copy_probs(b, j):
                if not real(b):
                    return
                act.wait_ge(probs_flipped, J * b.n + j + 1)
                wait(act, attn_done, J * b.n + j - 1)
                nc.scalar.activation(probs_t[:, j % 2, :], flipped[j % 2][:], ACT.Copy).then_inc(probs_t_ready, 1)

            def router_input(b):
                if not real(b):
                    return
                act.wait_ge(xn2_flipped, b.n + 1)
                wait(act, logits_ready, b.n)
                col = slice(b.n, b.n + 1) if isinstance(b.n, int) else bass.ds(b.n, 1)
                nc.scalar.activation(h2_t[:], side[0][:], ACT.Identity, bias=shift2[:, col],
                                     scale=scale2[:, col]).then_inc(h2t_ready, 1)

            def copy_x1(b):
                if not real(b):
                    return
                act.wait_ge(x1_ready, J * b.n + J)
                wait(act, scattered[b.p], 16 * J * b.h)
                n = slice(b.n, b.n + 1) if isinstance(b.n, int) else bass.ds(b.n, 1)
                nc.scalar.activation(payload[:, b.p, :, ROW_X1:ROW_X1 + H],
                                     x_all[:, n, :].rearrange("p b (j h) -> p (b j) h", j=J),
                                     ACT.Copy).then_inc(x1_copied, 1)

            def logit_exp(b):
                if not real(b):
                    return
                act.wait_ge(logit_ready, b.n + 1)
                nc.scalar.activation(logit_e[:], logit[:], ACT.Exp, scale=-1.0).then_inc(logit_e_ready, 1)

            def gates(b):
                if not real(b):
                    return
                act.wait_ge(mask_ready, b.n + 1)
                act.wait_ge(mod_loaded[b.p], 16 * (b.h + 1))
                n = slice(b.n, b.n + 1) if isinstance(b.n, int) else bass.ds(b.n, 1)
                for j in range(J):
                    last = nc.scalar.activation(payload[:, b.p, j, ROW_GATE:ROW_GATE + H],
                                                mod_all[:, n, 3 * H:4 * H].rearrange("p b h -> p (b h)"),
                                                ACT.Copy, scale=route_max[:, b.p, j:j + 1])
                last.then_inc(gates_ready, 1)

            def slot(i, k):
                now, after, prev = batch_at(i, k), batch_at(i, k + 1), batch_at(i, k - 1)
                exps(now, 1)
                copy_probs(now, 0)
                query(after)
                exps(now, 2)
                copy_probs(now, 1)
                copy_x1(prev)
                exps(now, 3)
                router_input(prev)
                copy_probs(now, 2)
                input_t(batch_at(i, k + 2))
                exps(after, 0)
                logit_exp(prev)
                copy_probs(now, 3)
                gates(prev)
                if isinstance(i, int) and k == -1:
                    for e in range(2):
                        load_w1(e)
                if isinstance(i, int) and 0 <= k < 2:
                    for e in range(3 * k + 2, 3 * k + 5):
                        load_w1(e)
                    if k == 1:
                        act.dma_start(w2_sb[:].rearrange("p (e k h) -> p e k h", e=E, k=KF),
                                      W2.rearrange("e (k p) h -> p e k h", p=P)).then_inc(w2_loaded, 16)

            attention_slots(act, slot)

            def split_hi(i, k):
                t = RING * i + k
                if not real_tile(t):
                    return
                act.wait_ge(f_flipped, t + 1)
                wait(act, up_done, t - 1)
                nc.scalar.activation(f_hi[:, k % 2, :], side[k % 2][:, 0:P], ACT.Copy).then_inc(f_hi_ready, 1)

            def gelu(i, k):
                t = RING * i + k
                if not real_tile(t):
                    return
                act.wait_ge(up_done, t + 1)
                wait(act, gelu_flipped, t - 1)
                nc.scalar.activation(probs[:, k % 2, :], scores[k % 2][:], ACT.Gelu).then_inc(gelu_done, 1)

            def ffn_slot(i, k):
                split_hi(i, k + 2)
                gelu(i, k + 1)

            ffn_slots(act, ffn_slot)

        @block.vector
        def _(dve):
            dve.wait_ge(s_cond_e, 1)
            nc.vector.tensor_scalar_add(cond_d[:], cond_e[:], 1.0).then_inc(s_dve0, 1)
            dve.wait_ge(s_dve0, 1)
            nc.vector.reciprocal(cond_s[:], cond_d[:]).then_inc(s_dve0, 1)
            dve.wait_ge(s_dve0, 2)
            nc.vector.tensor_tensor(silu[:], cond[:], cond_s[:], ALU.mult).then_inc(s_silu, 1)
            dve.wait_ge(s_silu_tp, 1)
            nc.vector.tensor_copy(silu_t[:], side[0][:, 0:B]).then_inc(s_silu_t, 1)
            dve.wait_ge(s_cols, 1)
            nc.vector.tensor_copy(shift1[:], side[1][:, 0:B]).then_inc(s_dve0, 1)
            nc.vector.tensor_scalar_add(scale1[:], side[1][:, B:2 * B], 1.0).then_inc(s_dve0, 1)
            nc.vector.tensor_copy(shift2[:], side[1][:, 2 * B:3 * B]).then_inc(s_dve0, 1)
            nc.vector.tensor_scalar_add(scale2[:], side[1][:, 3 * B:4 * B], 1.0).then_inc(s_dve0, 1)
            dve.wait_ge(s_rowsp, 1)
            for n, at in enumerate((0, 3)):
                g = mixed[1][0:B, at * H:(at + 1) * H]
                nc.vector.tensor_scalar(gate_sign[:, n * H:(n + 1) * H], g, 0.0, 2.0, ALU.is_ge, ALU.mult
                                        ).then_inc(s_dve0, 1)
                nc.vector.tensor_scalar_mul(gate_neg[:, n * H:(n + 1) * H], g, -1.0).then_inc(s_dve0, 1)
            nc.vector.tensor_scalar_add(mod_rows[:, H:2 * H], mixed[1][0:B, H:2 * H], 1.0).then_inc(s_dve0, 1)
            nc.vector.tensor_copy(mod_rows[:, 2 * H:3 * H], mixed[1][0:B, 2 * H:3 * H]).then_inc(s_dve0, 1)
            dve.wait_ge(s_dve0, 12)
            for n, at in enumerate((0, 3)):
                last = nc.vector.scalar_tensor_tensor(gate_size[:, n * H:(n + 1) * H],
                                                      mixed[1][0:B, at * H:(at + 1) * H], 0.25,
                                                      gate_neg[:, n * H:(n + 1) * H], ALU.max, ALU.max)
            last.then_inc(s_dve0, 1)
            dve.wait_ge(s_dve0, 13)
            for n, at in enumerate((0, 3)):
                last = nc.vector.scalar_tensor_tensor(mod_rows[:, at * H:(at + 1) * H],
                                                      gate_sign[:, n * H:(n + 1) * H], -1.0,
                                                      gate_size[:, n * H:(n + 1) * H], ALU.add, ALU.mult)
            last.then_inc(s_mod, 1)
            dve.wait_ge(s_consts, 5)
            nc.vector.tensor_copy(region[:], region_i[:])
            nc.vector.tensor_copy(order[:], order_i[:])
            nc.vector.tensor_copy(tile_no[:], tile_i[:]).then_inc(s_dve0, 1)
            nc.vector.memset(seen[:], 0.0).then_inc(seen_ready, 1)

            def x_of(b, j=None):
                n = slice(b.n, b.n + 1) if isinstance(b.n, int) else bass.ds(b.n, 1)
                x = x_all[:, n, :].rearrange("p b f -> p (b f)")
                return x if j is None else x[:, j * H:(j + 1) * H]

            def mod_of(b, part):
                n = slice(b.n, b.n + 1) if isinstance(b.n, int) else bass.ds(b.n, 1)
                return mod_all[:, n, part * H:(part + 1) * H].to_broadcast([P, J, H])

            def ln1(b, tiles):
                if not real(b):
                    return
                if tiles[0] == 0:
                    wait_apart(dve, x_loaded[b.p], 16 * (b.h + 1))
                for j in tiles:
                    nc.vector.bn_stats(stats1[:, b.p, j, :], x_of(b, j)).then_inc(ln1_stats, 1)
                for j in tiles:
                    wait_apart(dve, ln1_stats, J * b.n + j + 1)
                    nc.vector.bn_aggr(moments1[:, b.p, j, :], stats1[:, b.p, j, :]).then_inc(ln1_moments, 1)
                if tiles[-1] == J - 1:
                    dve.wait_ge(ln1_moments, J * b.n + J)
                    nc.vector.tensor_scalar_add(var1[:, b.p, :], moments1[:, b.p, :, 1], EPS).then_inc(var1_ready, 1)

            def normalize1(b):
                if not real(b):
                    return
                dve.wait_ge(rstd1_ready, b.n + 1)
                wait(dve, xn_flipped, b.n)
                for j in range(J):
                    last = nc.vector.tensor_scalar(xn[:, j, :], x_of(b, j), moments1[:, b.p, j, 0:1],
                                                   rstd1[:, b.p, j:j + 1], ALU.subtract, ALU.mult)
                last.then_inc(xn_ready, 1)

            def split_q(b):
                if not real(b):
                    return
                dve.wait_ge(q_ready, b.n + 1)
                nc.vector.tensor_copy(q_hi[:, b.p, :], q_t[:, b.p, :]).then_inc(q_hi_ready, 1)
                dve.wait_ge(q_hi_ready, b.n + 1)
                nc.vector.tensor_sub(q_lo[:, b.p, :], q_t[:, b.p, :], q_hi[:, b.p, :].bitcast(F32)
                                     ).then_inc(q_split, 1)

            def values(b):
                if not real(b):
                    return
                dve.wait_ge(v_flipped, b.n + 1)
                dve.wait_ge(mod_loaded[b.p], 16 * (b.h + 1))
                nc.vector.tensor_tensor(v_sb[:, b.p, :, :], side[1][:].rearrange("p (j h) -> p j h", j=J),
                                        mod_of(b, 0), ALU.mult).then_inc(v_ready, 1)

            def find_max(b, j):
                if not real(b):
                    return
                dve.wait_ge(scores_ready, J * b.n + j + 1)
                c = b.p * J + j
                nc.vector.tensor_reduce(row_max[:, c:c + 1], scores[j % 2][:], AX_X, ALU.max, negate=True
                                        ).then_inc(max_found, 1)
                dve.wait_ge(max_found, J * b.n + j + 1)
                nc.vector.tensor_scalar_mul(neg_max[:, c:c + 1], row_max[:, c:c + 1], SCALE).then_inc(max_ready, 1)

            def residual(b, j):
                if not real(b):
                    return
                dve.wait_ge(attn_done, J * b.n + j + 1)
                c = b.p * J + j
                nc.vector.reciprocal(den_inv[:, c:c + 1], den[:, c:c + 1]).then_inc(den_ready, 1)
                dve.wait_ge(den_ready, J * b.n + j + 1)
                nc.vector.scalar_tensor_tensor(x_of(b, j), mixed[j % 2][:, 0:H], den_inv[:, c:c + 1], x_of(b, j),
                                               ALU.mult, ALU.add).then_inc(x1_ready, 1)

            def ln2(b, j):
                if not real(b):
                    return
                wait_apart(dve, x1_ready, J * b.n + j + 1)
                nc.vector.bn_stats(stats2[:, b.p, j, :], x_of(b, j)).then_inc(ln2_stats, 1)
                wait_apart(dve, ln2_stats, J * b.n + j + 1)
                nc.vector.bn_aggr(moments2[:, b.p, j, :], stats2[:, b.p, j, :]).then_inc(ln2_moments, 1)
                if j == J - 1:
                    dve.wait_ge(ln2_moments, J * b.n + J)
                    nc.vector.tensor_scalar_add(var2[:, b.p, :], moments2[:, b.p, :, 1], EPS).then_inc(var2_ready, 1)

            def normalize2(b):
                if not real(b):
                    return
                dve.wait_ge(rstd2_ready, b.n + 1)
                wait(dve, xn2_flipped, b.n)
                wait(dve, h2_ready, b.n)
                for j in range(J):
                    last = nc.vector.tensor_scalar(xn2[:, j, :], x_of(b, j), moments2[:, b.p, j, 0:1],
                                                   rstd2[:, b.p, j:j + 1], ALU.subtract, ALU.mult)
                last.then_inc(xn2_ready, 1)

            def add_bias(b):
                if not real(b):
                    return
                dve.wait_ge(logits_ready, b.n + 1)
                nc.vector.tensor_tensor(logit[:].rearrange("p (j e) -> p j e", e=E),
                                        side[0][:, 0:J * E].rearrange("p (j e) -> p j e", e=E),
                                        br_sb[:].unsqueeze(1).to_broadcast([P, J, E]), ALU.add
                                        ).then_inc(logit_ready, 1)

            def choose(b):
                if not real(b):
                    return
                links = [0]

                def link(ins):
                    links[0] += 1
                    ins.then_inc(route_link, 1)
                    dve.wait_ge(route_link, 6 * b.n + links[0])

                def wide(a):
                    return a.unsqueeze(2).to_broadcast([P, J, E])

                dve.wait_ge(logit_e_ready, b.n + 1)
                wait(dve, gates_ready, b.n - 1)
                link(nc.vector.tensor_scalar_add(logit_d[:], logit_e[:], 1.0))
                link(nc.vector.reciprocal(route[:].rearrange("p j e -> p (j e)"), logit_d[:]))
                link(nc.vector.tensor_reduce(route_max[:, b.p, :], route[:], AX_X, ALU.max))
                link(nc.vector.tensor_tensor(at_max[:], route[:], wide(route_max[:, b.p, :]), ALU.is_equal))
                link(nc.vector.tensor_tensor(ranked[:], at_max[:], order[:].unsqueeze(1).to_broadcast([P, J, E]),
                                             ALU.mult))
                link(nc.vector.tensor_reduce(rank_max[:], ranked[:], AX_X, ALU.max))
                assert links[0] == 6
                nc.vector.tensor_tensor(mask[:], ranked[:], wide(rank_max[:]), ALU.is_equal).then_inc(mask_ready, 1)

            def choose_slots(b):
                if not real(b):
                    return
                dve.wait_ge(places_ready, b.n + 1)
                nc.vector.tensor_tensor(place[:], side[0][:, 0:J * E].rearrange("p (j e) -> p j e", e=E),
                                        region[:, 0:E].unsqueeze(1).to_broadcast([P, J, E]), ALU.add
                                        ).then_inc(place_link, 1)
                nc.vector.tensor_reduce(batch_count[:], mask[:].rearrange("p j e -> p e j"), AX_X, ALU.add
                                        ).then_inc(place_link, 1)
                dve.wait_ge(place_link, 3 * b.n + 1)
                nc.vector.tensor_tensor(placed[:], place[:], mask[:], ALU.mult).then_inc(place_link, 1)
                dve.wait_ge(place_link, 3 * b.n + 3)
                wait(dve, scattered[b.p], 16 * J * b.h)
                with nc.allow_low_precision("row numbers below 2^24 are exact"):
                    nc.vector.tensor_reduce(slots[:, b.p * J:(b.p + 1) * J], placed[:], AX_X, ALU.add
                                            ).then_inc(slots_ready, 1)
                    nc.vector.tensor_tensor(seen[:], seen[:], batch_count[:], ALU.add).then_inc(seen_ready, 1)

            def slot(i, k):
                now, after, prev = batch_at(i, k), batch_at(i, k + 1), batch_at(i, k - 1)
                find_max(now, 1)
                residual(prev, 3)
                ln2(prev, 3)
                choose_slots(batch_at(i, k - 2))
                ln1(batch_at(i, k + 2), (0, 1))
                find_max(now, 2)
                split_q(after)
                residual(now, 0)
                normalize2(prev)
                ln2(now, 0)
                ln1(batch_at(i, k + 2), (2, 3))
                find_max(now, 3)
                values(after)
                residual(now, 1)
                ln2(now, 1)
                normalize1(batch_at(i, k + 2))
                find_max(after, 0)
                add_bias(prev)
                residual(now, 2)
                ln2(now, 2)
                choose(prev)

            attention_slots(dve, slot)

            done = [0]

            def step(ins):
                done[0] += 1
                ins.then_inc(plan_link, 1)
                dve.wait_ge(plan_link, done[0])

            dve.wait_ge(counts_ready, 1)
            step(nc.vector.tensor_copy(counts[:], side[1][:, 0:E]))
            nc.vector.tensor_tensor(tail_row[:], counts[0:1, :], region[0:1, 0:E], ALU.add).then_inc(tails_ready, 1)
            step(nc.vector.tensor_scalar_add(padded_i[:], counts[:], float(P - 1)))
            step(nc.vector.tensor_single_scalar(tiles_i[:], padded_i[:], 7, ALU.arith_shift_right))
            step(nc.vector.tensor_copy(n_tiles[:], tiles_i[:]))
            nc.vector.memset(one_row[:], 1.0)
            step(nc.vector.memset(tiles_to[:, 0:1], 0.0))
            step(nc.vector.tensor_tensor_scan(tiles_to[:, 1:E + 1], one_row[:], n_tiles[:], 0.0,
                                              ALU.mult, ALU.add))
            step(nc.vector.scalar_tensor_tensor(base[:], tiles_to[:], -float(P), region[:], ALU.mult, ALU.add))
            step(nc.vector.tensor_tensor(base_step[:], base[:, 1:E + 1], base[:, 0:E], ALU.subtract))
            step(nc.vector.tensor_tensor(passed[:], tile_no[:].unsqueeze(2).to_broadcast([1, TILES, E]),
                                         tiles_to[0:1, 1:E + 1].unsqueeze(1).to_broadcast([1, TILES, E]), ALU.is_ge))
            step(nc.vector.tensor_reduce(owner[:], passed[:], AX_X, ALU.add))
            step(nc.vector.tensor_tensor(steps[:], passed[:],
                                         base_step[0:1, :].unsqueeze(1).to_broadcast([1, TILES, E]), ALU.mult))
            step(nc.vector.tensor_reduce(start[:], steps[:], AX_X, ALU.add))
            step(nc.vector.scalar_tensor_tensor(start_f[:], tile_no[:], float(P), start[:], ALU.mult, ALU.add))
            step(nc.vector.tensor_scalar(owner[:], owner[:], float(E - 1), float(F), ALU.min, ALU.mult))
            step(nc.vector.tensor_scalar(tile_row[:], start_f[:], float(E * REGION), None, ALU.min))
            nc.vector.tensor_copy(tile_weights[:], owner[:]).then_inc(plan_ready, 1)

            def split_lo(i, k):
                t = RING * i + k
                if not real_tile(t):
                    return
                dve.wait_ge(f_hi_ready, t + 1)
                nc.vector.tensor_sub(f_lo[:, k % 2, :], side[k % 2][:, 0:P], f_hi[:, k % 2, :].bitcast(F32)
                                     ).then_inc(f_split, 1)

            def copy_gelu(i, k):
                t = RING * i + k
                if not real_tile(t):
                    return
                dve.wait_ge(gelu_flipped, t + 1)
                wait(dve, down_done, t - 1)
                nc.vector.tensor_copy(probs_t[:, k % 2, :], flipped[k % 2][:]).then_inc(gelu_t_ready, 1)

            def finish(i, k):
                t = RING * i + k
                if not real_tile(t):
                    return
                r = k % RING
                dve.wait_ge(down_done, t + 1)
                nc.vector.tensor_tensor(gated[:, k % 2, :], mixed[k % 2][:, 0:H],
                                        rows[:, r, ROW_GATE:ROW_GATE + H], ALU.mult).then_inc(gated_ready, 1)
                dve.wait_ge(gated_ready, t + 1)
                wait(dve, y_scattered[r], 16 * (i + k // RING))
                nc.vector.tensor_tensor(y_out[:, r, :], gated[:, k % 2, :], rows[:, r, ROW_X1:ROW_X1 + H],
                                        ALU.add).then_inc(y_ready, 1)

            def ffn_slot(i, k):
                split_lo(i, k + 2)
                copy_gelu(i, k)
                finish(i, k - 1)

            ffn_slots(dve, ffn_slot)

        @block.gpsimd
        def _(pool):
            nc.gpsimd.memset(ident[:], 0.0).then_inc(s_pool, 1)
            nc.gpsimd.memset(upper[:], 1.0).then_inc(s_pool, 1)
            nc.gpsimd.memset(ones[:], 1.0)
            nc.gpsimd.memset(neg_half[:], -0.5)
            nc.gpsimd.memset(pad_rows[:], 0.0).then_inc(s_pool, 1)
            pool.wait_ge(s_pool, 3)
            nc.gpsimd.affine_select(out=ident[:], in_=ident[:], compare_op=ALU.not_equal, fill=1.0, base=0,
                                    pattern=[[-1, P]], channel_multiplier=1).then_inc(s_consts, 1)
            nc.gpsimd.affine_select(out=upper[:], in_=upper[:], compare_op=ALU.is_gt, fill=0.0, base=0,
                                    pattern=[[1, P]], channel_multiplier=-1).then_inc(s_consts, 1)
            nc.gpsimd.iota(region_i[:], pattern=[[REGION, E + 1]], base=0, channel_multiplier=0).then_inc(s_consts, 1)
            nc.gpsimd.iota(order_i[:], pattern=[[-1, E]], base=E, channel_multiplier=0).then_inc(s_consts, 1)
            nc.gpsimd.iota(tile_i[:], pattern=[[1, TILES]], base=0, channel_multiplier=0).then_inc(s_consts, 1)
            nc.gpsimd.iota(token_id[:], pattern=[[S, B], [1, J]], base=0, channel_multiplier=J)
            nc.gpsimd.iota(pad_rows[:, ROW_ID:ROW].bitcast(I32), pattern=[[0, ROW - ROW_ID]], base=N,
                           channel_multiplier=0).then_inc(s_pad0, 2)
            nc.gpsimd.memset(payload[:, :, :, ROW_ID:ROW], 0.0).then_inc(s_pool, 1)
            pool.wait_ge(s_pool, 4)

            def invert1(b):
                if not real(b):
                    return
                pool.wait_ge(var1_ready, b.n + 1)
                nc.gpsimd.tensor_tensor(rstd1[:, b.p, :], var1[:, b.p, :], neg_half[:], ALU.pow
                                        ).then_inc(rstd1_ready, 1)

            def invert2(b):
                if not real(b):
                    return
                pool.wait_ge(var2_ready, b.n + 1)
                nc.gpsimd.tensor_tensor(rstd2[:, b.p, :], var2[:, b.p, :], neg_half[:], ALU.pow
                                        ).then_inc(rstd2_ready, 1)

            def modulate(b):
                if not real(b):
                    return
                pool.wait_ge(xn2_ready, b.n + 1)
                pool.wait_ge(mod_loaded[b.p], 16 * (b.h + 1))
                wait(pool, scattered[b.p], 16 * J * b.h)
                n = slice(b.n, b.n + 1) if isinstance(b.n, int) else bass.ds(b.n, 1)
                h2 = payload[:, b.p, :, 0:H]
                nc.gpsimd.tensor_tensor(h2, xn2[:], mod_all[:, n, H:2 * H].to_broadcast([P, J, H]), ALU.mult
                                        ).then_inc(h2_scaled, 1)
                c = slice(b.n * J, (b.n + 1) * J) if isinstance(b.n, int) else bass.ds(b.n * J, J)
                nc.gpsimd.tensor_copy(payload[:, b.p, :, ROW_ID].bitcast(I32), token_id[:, c])
                pool.wait_ge(h2_scaled, b.n + 1)
                nc.gpsimd.tensor_tensor(h2, h2, mod_all[:, n, 2 * H:3 * H].to_broadcast([P, J, H]), ALU.add
                                        ).then_inc(h2_ready, 1)

            def scatter(b):
                if not real(b):
                    return
                wait_apart(pool, slots_ready, b.n + 1)
                pool.wait_ge(gates_ready, b.n + 1)
                pool.wait_ge(x1_copied, b.n + 1)
                pool.wait_ge(h2_ready, b.n + 1)
                for j in range(J):
                    c = b.p * J + j
                    nc.gpsimd.indirect_dma_start(
                        rows_dram, bass.IndirectOffsetOnAxis(ap=slots[:, c:c + 1], axis=0),
                        payload[:, b.p, j, :], None).then_inc(scattered[b.p], 16)

            def split_w1(e):
                pool.wait_ge(w1_loaded[e % 2], 16 * (e // 2 + 1))
                at = slice(e * F, (e + 1) * F)
                nc.gpsimd.tensor_copy(w1_hi[:, at], w1_raw[:, e % 2, :]).then_inc(w1_half, 1)
                pool.wait_ge(w1_half, e + 1)
                nc.gpsimd.tensor_sub(w1_lo[:, at], w1_raw[:, e % 2, :], w1_hi[:, at].bitcast(F32)
                                     ).then_inc(w1_split, 1)

            def slot(i, k):
                prev = batch_at(i, k - 1)
                invert2(prev)
                scatter(batch_at(i, k - 2))
                invert1(batch_at(i, k + 2))
                modulate(prev)
                if isinstance(i, int) and 0 <= k < 2:
                    for e in range(4 * k, 4 * k + 4):
                        split_w1(e)

            attention_slots(pool, slot)

            def write_out(i, k):
                t = RING * i + k
                if not real_tile(t):
                    return
                wait_apart(pool, y_ready, t + 1)
                nc.gpsimd.indirect_dma_start(
                    out_rows, bass.IndirectOffsetOnAxis(ap=rows[:, k % RING, ROW_ID:ROW_ID + 1].bitcast(I32), axis=0),
                    y_out[:, k % RING, :], None, bounds_check=N - 1, oob_is_err=False
                ).then_inc(y_scattered[k % RING], 16)

            def ffn_slot(i, k):
                write_out(i, k - 1)

            ffn_slots(pool, ffn_slot)


_INS = ["L0_attn_inputs", "L0_attn_Wq", "L0_attn_bq", "L0_ffn_Wr", "L0_ffn_br", "L0_ffn_W1", "L0_ffn_W2", "L0_c",
        "L0_wmod"]


def kernel(**inputs):
    import numpy as _np
    import concourse.bacc as _bacc
    from concourse import mybir as _mybir
    from concourse.bass_utils import run_bass_kernel_spmd as _run

    nc = _bacc.Bacc("TRN2", target_bir_lowering=False, num_devices=1)
    arrays, args = {}, []
    for name in _INS:
        a = _np.ascontiguousarray(inputs[name])
        arrays[f"in_{name}_dram"] = a
        args.append(nc.dram_tensor(f"in_{name}_dram", a.shape, _mybir.dt.from_np(a.dtype), kind="ExternalInput").ap())
    shape = arrays["in_L0_attn_inputs_dram"].shape
    args.append(nc.dram_tensor("out_0_dram", shape, _mybir.dt.float32, kind="ExternalOutput").ap())
    adaln_block(nc, *args)
    r = _run(nc, [arrays], core_ids=[0])
    return r.results[0]["out_0_dram"]
```

```python
from collections import namedtuple
from contextlib import ExitStack

import concourse.bass as bass
from concourse import mybir

P = 128
F32 = mybir.dt.float32
F32R = mybir.dt.float32r
BF16 = mybir.dt.bfloat16
I32 = mybir.dt.int32
ALU = mybir.AluOpType
ACT = mybir.ActivationFunctionType
AX_X = mybir.AxisListType.X
EPS = 1e-5

Batch = namedtuple("Batch", "n p h")


def batch_at(i, k):
    return Batch(2 * i + k, k % 2, i + k // 2)


def adaln_block(nc, x_in, Wq, bq, Wr, br, W1, W2, c_in, wmod, out):
    B, S, H = x_in.shape
    E, _, F = W1.shape
    J = S // P
    KF = F // P
    N = B * S
    SCALE = float(H) ** -0.5
    ROW = 3 * H + 4
    ROW_X1, ROW_GATE, ROW_ID = H, 2 * H, 3 * H
    REGION = N + P
    TILES = N // P + E - 1
    RING = 12
    assert H == P and J == 4 and F == 512

    rows_dram = nc.dram_tensor("sorted_rows", [E * REGION + P, ROW], F32).ap()
    gates_dram = nc.dram_tensor("stored_gates", [B, 2 * H], F32).ap()
    x_view = x_in.rearrange("b (p j) h -> b p (j h)", j=J)
    out_rows = out.rearrange("b s h -> (b s) h")

    with ExitStack() as ctx:
        def sb(name, shape, dt=F32):
            return ctx.enter_context(nc.sbuf_tensor(name, shape, dt))

        def sem(name):
            return ctx.enter_context(nc.semaphore(name))

        scores = [ctx.enter_context(nc.psum_tensor(f"scores{n}", [P, 512], F32)) for n in range(2)]
        flipped = [ctx.enter_context(nc.psum_tensor(f"flipped{n}", [P, 512], F32)) for n in range(2)]
        mixed = [ctx.enter_context(nc.psum_tensor(f"mixed{n}", [P, 512], F32)) for n in range(2)]
        side = [ctx.enter_context(nc.psum_tensor(f"side{n}", [P, 512], F32)) for n in range(2)]

        ident = sb("ident", [P, P])
        upper = sb("upper", [P, P], BF16)
        ones = sb("ones", [P, P], BF16)
        neg_half = sb("neg_half", [P, J])
        region_i = sb("region_i", [P, E + 1], I32)
        region = sb("region", [P, E + 1])
        order_i = sb("order_i", [P, E], I32)
        order = sb("order", [P, E])
        token_id = sb("token_id", [P, B * J], I32)
        tile_i = sb("tile_i", [1, TILES + 1], I32)
        tile_no = sb("tile_no", [1, TILES + 1])
        pad_rows = sb("pad_rows", [P, ROW])

        wq_sb = sb("wq_sb", [P, H])
        bq_sb = sb("bq_sb", [P, 1])
        wr_sb = sb("wr_sb", [P, E])
        br_sb = sb("br_sb", [P, E])
        w1_raw = sb("w1_raw", [P, E * F])
        w1_hi = sb("w1_hi", [P, E * F], F32R)
        w1_lo = sb("w1_lo", [P, E * F], F32R)
        w2_sb = sb("w2_sb", [P, E * F])
        cond = sb("cond", [B, H])
        cond_e = sb("cond_e", [B, H])
        cond_d = sb("cond_d", [B, H])
        cond_s = sb("cond_s", [B, H])
        silu = sb("silu", [B, H])
        silu_t = sb("silu_t", [P, B])
        wmod_sb = sb("wmod_sb", [P, 6 * H])
        shift1 = sb("shift1", [P, B])
        scale1 = sb("scale1", [P, B])
        shift2 = sb("shift2", [P, B])
        scale2 = sb("scale2", [P, B])
        gate_rows = sb("gate_rows", [B, 2 * H])
        gate_sign = sb("gate_sign", [B, 2 * H])
        gate_neg = sb("gate_neg", [B, 2 * H])
        gate_size = sb("gate_size", [B, 2 * H])
        gate1 = sb("gate1", [P, 2, H])
        gate2 = sb("gate2", [P, 2, H])

        x_raw = sb("x_raw", [P, 2, J, H])
        x_res = sb("x_res", [P, 2, J, H])
        x1 = sb("x1", [P, 2, J, H])
        stats1 = sb("stats1", [P, 2, J, 6])
        stats2 = sb("stats2", [P, 2, J, 6])
        moments1 = sb("moments1", [P, 2, J, 2])
        moments2 = sb("moments2", [P, 2, J, 2])
        var1 = sb("var1", [P, 2, J])
        var2 = sb("var2", [P, 2, J])
        rstd1 = sb("rstd1", [P, 2, J])
        rstd2 = sb("rstd2", [P, 2, J])
        neg_mean1 = sb("neg_mean1", [P, 2, J])
        offset1 = sb("offset1", [P, 2, J])
        xn = sb("xn", [P, J, H])
        h_t = sb("h_t", [P, J * P])
        q_t = sb("q_t", [P, 2, J * P])
        q_hi = sb("q_hi", [P, 2, J * P], F32R)
        q_lo = sb("q_lo", [P, 2, J * P], F32R)
        v_sb = sb("v_sb", [P, 2, J, H])
        row_max = sb("row_max", [P, 2 * J])
        neg_max = sb("neg_max", [P, 2 * J])
        den = sb("den", [P, 2 * J])
        den_inv = sb("den_inv", [P, 2 * J])
        probs = sb("probs", [P, 2, 512])
        probs_t = sb("probs_t", [P, 2, 512])
        xn2 = sb("xn2", [P, J, H])
        h2_t = sb("h2_t", [P, J * P])
        payload = sb("payload", [P, 2, J, ROW])
        logit = sb("logit", [P, J * E])
        logit_e = sb("logit_e", [P, J * E])
        logit_d = sb("logit_d", [P, J * E])
        least_d = sb("least_d", [P, J])
        route_max = sb("route_max", [P, J])
        at_max = sb("at_max", [P, J, E])
        ranked = sb("ranked", [P, J, E])
        rank_max = sb("rank_max", [P, J])
        mask = sb("mask", [P, J, E], BF16)
        place = sb("place", [P, J, E])
        placed = sb("placed", [P, J, E])
        slots = sb("slots", [P, 2 * J], I32)
        batch_count = sb("batch_count", [P, E])
        seen = sb("seen", [P, E], BF16)

        counts = sb("counts", [P, E])
        padded_i = sb("padded_i", [P, E], I32)
        tiles_i = sb("tiles_i", [P, E], I32)
        n_tiles = sb("n_tiles", [P, E])
        one_row = sb("one_row", [P, E])
        tiles_to = sb("tiles_to", [P, E + 1])
        base = sb("base", [P, E + 1])
        base_step = sb("base_step", [P, E])
        passed = sb("passed", [1, TILES + 1, E])
        steps = sb("steps", [1, TILES + 1, E])
        owner = sb("owner", [1, TILES + 1])
        start = sb("start", [1, TILES + 1])
        start_f = sb("start_f", [1, TILES + 1])
        tile_weights = sb("tile_weights", [1, TILES + 1], I32)
        tile_row = sb("tile_row", [1, TILES + 1], I32)
        tail_row = sb("tail_row", [1, E], I32)

        rows = sb("rows", [P, RING, ROW])
        y_out = sb("y_out", [P, RING, H])
        gelu_warm = sb("gelu_warm", [P, 1])
        f_hi = sb("f_hi", [P, 2, P], F32R)
        f_lo = sb("f_lo", [P, 2, P], F32R)
        tokens = sb("tokens", [P, RING], I32)
        gated = sb("gated", [P, 2, H])

        s_consts = sem("s_consts")
        s_pool = sem("s_pool")
        cond_loaded = sem("cond_loaded")
        s_small = sem("s_small")
        s_small2 = sem("s_small2")
        s_dve0 = sem("s_dve0")
        s_cond_e = sem("s_cond_e")
        s_silu = sem("s_silu")
        s_silu_tp = sem("s_silu_tp")
        s_silu_t = sem("s_silu_t")
        s_cols = sem("s_cols")
        s_rowsp = sem("s_rowsp")
        s_mod = sem("s_mod")
        s_mod_dram = sem("s_mod_dram")
        s_pad0 = sem("s_pad0")
        x_loaded = [sem(f"x_loaded{n}") for n in range(2)]
        x_res_loaded = [sem(f"x_res_loaded{n}") for n in range(2)]
        gate1_loaded = [sem(f"gate1_loaded{n}") for n in range(2)]
        gate2_loaded = [sem(f"gate2_loaded{n}") for n in range(2)]
        w1_loaded = sem("w1_loaded")
        w2_loaded = sem("w2_loaded")
        w1_split = sem("w1_split")
        w1_half = sem("w1_half")
        ln1_stats = sem("ln1_stats")
        ln1_moments = sem("ln1_moments")
        var1_ready = sem("var1_ready")
        rstd1_ready = sem("rstd1_ready")
        offset1_ready = sem("offset1_ready")
        xn_ready = sem("xn_ready")
        xn_flipped = sem("xn_flipped")
        h_ready = sem("h_ready")
        q_projected = sem("q_projected")
        q_ready = sem("q_ready")
        q_hi_ready = sem("q_hi_ready")
        q_split = sem("q_split")
        v_flipped = sem("v_flipped")
        v_ready = sem("v_ready")
        scores_ready = sem("scores_ready")
        max_found = sem("max_found")
        max_ready = sem("max_ready")
        exp_done = sem("exp_done")
        probs_flipped = sem("probs_flipped")
        probs_t_ready = sem("probs_t_ready")
        attn_done = sem("attn_done")
        den_ready = sem("den_ready")
        x1_ready = sem("x1_ready")
        ln2_stats = sem("ln2_stats")
        ln2_moments = sem("ln2_moments")
        var2_ready = sem("var2_ready")
        rstd2_ready = sem("rstd2_ready")
        xn2_ready = sem("xn2_ready")
        xn2_flipped = sem("xn2_flipped")
        h2t_ready = sem("h2t_ready")
        logits_ready = sem("logits_ready")
        logit_ready = sem("logit_ready")
        logit_e_ready = sem("logit_e_ready")
        route_link = sem("route_link")
        probability_ready = sem("probability_ready")
        mask_ready = sem("mask_ready")
        places_ready = sem("places_ready")
        place_link = sem("place_link")
        slots_ready = sem("slots_ready")
        seen_ready = sem("seen_ready")
        x1_copied = sem("x1_copied")
        gates_ready = sem("gates_ready")
        h2_flipped = sem("h2_flipped")
        h2_ready = sem("h2_ready")
        scattered = [sem(f"scattered{n}") for n in range(2)]
        counts_ready = sem("counts_ready")
        plan_link = sem("plan_link")
        plan_ready = sem("plan_ready")
        tails_ready = sem("tails_ready")
        tails_filled = sem("tails_filled")
        rows_loaded = [sem(f"rows_loaded{n}") for n in range(RING)]
        f_flipped = sem("f_flipped")
        f_hi_ready = sem("f_hi_ready")
        f_split = sem("f_split")
        up_done = sem("up_done")
        gelu_done = sem("gelu_done")
        gelu_flipped = sem("gelu_flipped")
        gelu_t_ready = sem("gelu_t_ready")
        down_done = sem("down_done")
        gated_ready = sem("gated_ready")
        tokens_kept = sem("tokens_kept")
        y_ready = sem("y_ready")
        y_scattered = [sem(f"y_scattered{n}") for n in range(RING)]

        def wait(eng, s, value):
            if not isinstance(value, int) or value > 0:
                eng.wait_ge(s, value)

        def wait_apart(eng, s, value):
            if not isinstance(value, int):
                value = eng.to_reg(value)
                eng.wait_ge(x_loaded[0], 16)
            wait(eng, s, value)

        def real(b):
            return not isinstance(b.n, int) or 0 <= b.n < B

        LOOP_FROM, LOOP_TO = 1, B // 2 - 1

        def attention_slots(eng, slot, loop_to=LOOP_TO):
            for k in range(-2, 2 * LOOP_FROM):
                slot(0, k)
            with eng.Fori(LOOP_FROM, loop_to) as i:
                for k in range(2):
                    slot(i, k)
            for k in range(2 * loop_to, B + 3):
                slot(0, k)

        FFN_FROM, FFN_TO = 1, (TILES - 2) // RING

        def ffn_slots(eng, slot):
            for k in range(-2, RING * FFN_FROM):
                slot(0, k)
            with eng.Fori(FFN_FROM, FFN_TO) as i:
                for k in range(RING):
                    slot(i, k)
            for k in range(RING * FFN_TO, TILES + 1):
                slot(0, k)

        def real_tile(t):
            return not isinstance(t, int) or 0 <= t < TILES

        W1_SPLITS = {k: range(k * E // 2, (k + 1) * E // 2) for k in range(2)}

        block = ctx.enter_context(nc.Block())

        def fill_tails(eng, engine_type, experts):
            eng.wait_ge(tails_ready, 1)
            _, firsts = nc.values_load_multi_w_load_instructions(
                tail_row[0:1, experts[0]:experts[-1] + 1], engines=[engine_type],
                min_val=0, max_val=(E - 1) * REGION + N)
            for first in firsts:
                eng.dma_start(rows_dram[bass.ds(first, P), :], pad_rows[:]).then_inc(tails_filled, 16)

        @block.sync
        def _(sp):
            def row(b):
                return slice(b.n, b.n + 1) if isinstance(b.n, int) else bass.ds(b.n, 1)

            def load_x(b):
                if not real(b):
                    return
                wait_apart(sp, xn_ready, b.n - 1)
                sp.dma_start(x_raw[:, b.p:b.p + 1, :, :].rearrange("p b j h -> p b (j h)"),
                             x_view[row(b)].rearrange("b p f -> p b f")
                             ).then_inc(x_loaded[b.p], 16)

            def load_x_again(b):
                if not real(b):
                    return
                wait_apart(sp, x1_ready, J * (b.n - 1))
                sp.dma_start(x_res[:, b.p:b.p + 1, :, :].rearrange("p b j h -> p b (j h)"),
                             x_view[row(b)].rearrange("b p f -> p b f")
                             ).then_inc(x_res_loaded[b.p], 16)

            def load_gate1(b):
                if not real(b):
                    return
                wait_apart(sp, v_ready, b.n - 1)
                sp.dma_start(gate1[:, b.p:b.p + 1, :], gates_dram[row(b), 0:H].unsqueeze(0).to_broadcast([P, 1, H])
                             ).then_inc(gate1_loaded[b.p], 16)

            def load_gate2(b):
                if not real(b):
                    return
                wait_apart(sp, gates_ready, b.n - 1)
                sp.dma_start(gate2[:, b.p:b.p + 1, :], gates_dram[row(b), H:2 * H].unsqueeze(0).to_broadcast([P, 1, H])
                             ).then_inc(gate2_loaded[b.p], 16)

            sp.dma_start(cond[:], c_in).then_inc(cond_loaded, 16)
            sp.dma_start(wmod_sb[:], wmod).then_inc(s_small2, 16)
            for n in range(2):
                load_x(batch_at(0, n))
            sp.wait_ge(s_mod, 1)
            sp.dma_start(gates_dram, gate_rows[:]).then_inc(s_mod_dram, 16)
            sp.wait_ge(s_mod_dram, 16)
            load_gate1(batch_at(0, 0))

            def slot(i, k):
                load_x(batch_at(i, k + 4))
                load_gate1(batch_at(i, k + 3))
                load_gate2(batch_at(i, k))
                load_x_again(batch_at(i, k + 1))
                if isinstance(i, int) and k == -1:
                    sp.dma_start(w1_raw[:].rearrange("h (e f) -> h e f", f=F), W1.rearrange("e h f -> h e f")
                                 ).then_inc(w1_loaded, 16)
                if isinstance(i, int) and k == B - 2:
                    sp.dma_start(w2_sb[:].rearrange("p (e k h) -> p e k h", e=E, k=KF),
                                 W2.rearrange("e (k p) h -> p e k h", p=P)).then_inc(w2_loaded, 16)

            attention_slots(sp, slot, LOOP_TO - 1)
            sp.wait_ge(s_pad0, 2)
            sp.dma_start(rows_dram[E * REGION:, :], pad_rows[:]).then_inc(tails_filled, 16)
            fill_tails(sp, mybir.EngineType.SP, range(0, E // 2))
            sp.wait_ge(plan_ready, 1)
            _, first_rows = nc.values_load_multi_w_load_instructions(
                tile_row[0:1, 1:1 + RING], engines=[mybir.EngineType.SP], min_val=0, max_val=E * REGION)
            for n in range(2):
                sp.wait_ge(scattered[n], 16 * J * (B // 2))
            sp.wait_ge(tails_filled, 16 * (E + 1))

            def load(i, k):
                t = RING * i + k
                wait(sp, y_ready, t - RING + 1)
                at = bass.ds(t + 1, 1) if not isinstance(t, int) else slice(t + 1, t + 2)
                first = sp.value_load(tile_row[0:1, at], min_val=0, max_val=E * REGION)
                sp.dma_start(rows[:, k % RING, :], rows_dram[bass.ds(first, P), :]
                             ).then_inc(rows_loaded[k % RING], 16)

            for k, first in enumerate(first_rows):
                sp.dma_start(rows[:, k, :], rows_dram[bass.ds(first, P), :]).then_inc(rows_loaded[k], 16)
            with sp.Fori(1, TILES // RING) as i:
                for k in range(RING):
                    load(i, k)
            for k in range(RING * (TILES // RING), TILES):
                load(0, k)
            for k in range(RING):
                sp.wait_ge(y_scattered[k], 16 * ((TILES - k + RING - 1) // RING))

        @block.tensor
        def _(pe):
            pe.wait_ge(s_silu, 1)
            pe.wait_ge(s_consts, 1)
            nc.tensor.transpose(side[0][:, 0:B], silu[:], ident[0:B, 0:B]).then_inc(s_silu_tp, 1)
            pe.wait_ge(s_silu_t, 1)
            pe.wait_ge(s_small2, 16)
            for n, part in enumerate((0, 1, 3, 4)):
                last = nc.tensor.matmul(side[1][:, n * B:(n + 1) * B], wmod_sb[:, part * H:(part + 1) * H],
                                        silu_t[:], start=True, stop=True)
            last.then_inc(s_cols, 1)
            for n, part in enumerate((2, 5)):
                last = nc.tensor.matmul(mixed[1][0:B, n * H:(n + 1) * H], silu_t[:],
                                        wmod_sb[:, part * H:(part + 1) * H], start=True, stop=True)
            last.then_inc(s_rowsp, 1)

            def flip_xn(b):
                if not real(b):
                    return
                pe.wait_ge(xn_ready, b.n + 1)
                if isinstance(b.n, int) and b.n == 0:
                    pe.wait_ge(s_dve0, 6)
                wait(pe, v_ready, b.n)
                for j in range(J):
                    last = nc.tensor.transpose(side[1][:, j * P:(j + 1) * P], xn[:, j, :], ident[:])
                last.then_inc(xn_flipped, 1)

            def project(b):
                if not real(b):
                    return
                pe.wait_ge(h_ready, b.n + 1)
                if isinstance(b.n, int) and b.n == 0:
                    pe.wait_ge(s_small, 64)
                nc.tensor.matmul(side[1][:], wq_sb[:], h_t[:], start=True, stop=True).then_inc(q_projected, 1)

            def flip_v(b):
                if not real(b):
                    return
                pe.wait_ge(q_ready, b.n + 1)
                pe.wait_ge(q_hi_ready, b.n + 1)
                for j in range(J):
                    last = nc.tensor.transpose(side[1][:, j * P:(j + 1) * P],
                                               q_t[:, b.p, j * P:(j + 1) * P], ident[:])
                last.then_inc(v_flipped, 1)

            def score(b, j):
                if not real(b):
                    return
                if j == 0:
                    pe.wait_ge(q_split, b.n + 1)
                wait(pe, exp_done, J * b.n + j - 1)
                mine = slice(j * P, (j + 1) * P)
                o = scores[j % 2][:]
                nc.tensor.matmul(o, q_lo[:, b.p, mine], q_hi[:, b.p, :], start=True, stop=False)
                nc.tensor.matmul(o, q_hi[:, b.p, mine], q_lo[:, b.p, :], start=False, stop=False)
                nc.tensor.matmul(o, q_hi[:, b.p, mine], q_hi[:, b.p, :], start=False, stop=True
                                 ).then_inc(scores_ready, 1)

            def flip_probs(b, j):
                if not real(b):
                    return
                pe.wait_ge(exp_done, J * b.n + j + 1)
                wait(pe, probs_t_ready, J * b.n + j - 1)
                for k in range(J):
                    last = nc.tensor.transpose(flipped[j % 2][:, k * P:(k + 1) * P],
                                               probs[:, j % 2, k * P:(k + 1) * P], ident[:])
                last.then_inc(probs_flipped, 1)

            def mix(b, j):
                if not real(b):
                    return
                pe.wait_ge(probs_t_ready, J * b.n + j + 1)
                if j == 0:
                    pe.wait_ge(v_ready, b.n + 1)
                wait(pe, x1_ready, J * b.n + j - 1)
                for k in range(J):
                    last = nc.tensor.matmul(mixed[j % 2][:, 0:H], probs_t[:, j % 2, k * P:(k + 1) * P],
                                            v_sb[:, b.p, k, :], start=(k == 0), stop=(k == J - 1))
                last.then_inc(attn_done, 1)

            def flip_xn2(b):
                if not real(b):
                    return
                pe.wait_ge(xn2_ready, b.n + 1)
                if not isinstance(b.n, int) or b.n > 0:
                    pe.wait_ge(place_link, 3 * (b.n - 1) + 1)
                for j in range(J):
                    last = nc.tensor.transpose(side[0][:, j * P:(j + 1) * P], xn2[:, j, :], ident[:])
                last.then_inc(xn2_flipped, 1)

            def router(b):
                if not real(b):
                    return
                pe.wait_ge(h2t_ready, b.n + 1)
                for j in range(J):
                    last = nc.tensor.matmul(side[0][:, j * E:(j + 1) * E], h2_t[:, j * P:(j + 1) * P],
                                            wr_sb[:], start=True, stop=True)
                last.then_inc(logits_ready, 1)

            def flip_h2(b):
                if not real(b):
                    return
                pe.wait_ge(logit_ready, b.n + 1)
                for j in range(J):
                    last = nc.tensor.transpose(side[0][:, j * P:(j + 1) * P], h2_t[:, j * P:(j + 1) * P],
                                               ident[:])
                last.then_inc(h2_flipped, 1)

            def places(b):
                if not real(b):
                    return
                pe.wait_ge(mask_ready, b.n + 1)
                pe.wait_ge(seen_ready, b.n + 1)
                pe.wait_ge(h2_ready, b.n + 1)
                o = side[0][:, 0:J * E].rearrange("p (j e) -> p j e", e=E)
                nc.tensor.matmul(o, upper[:], mask[:], start=True, stop=False)
                nc.tensor.matmul(o, ones[:], seen[:].unsqueeze(1).to_broadcast([P, J, E]),
                                 start=False, stop=False)
                for d in range(1, J):
                    last = nc.tensor.matmul(o[:, d:J, :], ones[:], mask[:, 0:J - d, :],
                                            start=False, stop=(d == J - 1))
                last.then_inc(places_ready, 1)

            def slot(i, k):
                before2, before, now, after, after2 = (batch_at(i, k + d) for d in range(-2, 3))
                score(now, 1)
                flip_probs(now, 0)
                mix(before, 3)
                project(after)
                score(now, 2)
                router(before2)
                flip_probs(now, 1)
                mix(now, 0)
                score(now, 3)
                flip_v(after)
                flip_h2(before2)
                flip_probs(now, 2)
                mix(now, 1)
                score(after, 0)
                flip_probs(now, 3)
                places(before2)
                mix(now, 2)
                flip_xn(after2)
                flip_xn2(before)

            attention_slots(pe, slot)
            pe.wait_ge(seen_ready, B + 1)
            nc.tensor.matmul(side[1][:, 0:E], ones[:], seen[:], start=True, stop=True).then_inc(counts_ready, 1)

            def load_weights_of(i, first, count):
                t = RING * i + first
                _, regs = nc.values_load_multi_w_load_instructions(
                    tile_weights[0:1, bass.ds(t + 1, count)], engines=[mybir.EngineType.PE],
                    min_val=0, max_val=(E - 1) * F)
                return dict(zip(range(first, first + count), regs))

            def flip_rows(i, k):
                t = RING * i + k
                if not real_tile(t):
                    return
                pe.wait_ge(rows_loaded[k % RING], 16 * (i + k // RING + 1))
                wait(pe, f_split, t - 1)
                nc.tensor.transpose(side[k % 2][:, 0:P], rows[:, k % RING, 0:H], ident[:]).then_inc(f_flipped, 1)

            def up(i, k, weights):
                t = RING * i + k
                if not real_tile(t):
                    return
                w = weights[k]
                pe.wait_ge(f_split, t + 1)
                wait(pe, gelu_done, t - 1)
                o = scores[k % 2][:]
                nc.tensor.matmul(o, f_lo[:, k % 2, :], w1_hi[:, bass.ds(w, F)], start=True, stop=False)
                nc.tensor.matmul(o, f_hi[:, k % 2, :], w1_lo[:, bass.ds(w, F)], start=False, stop=False)
                nc.tensor.matmul(o, f_hi[:, k % 2, :], w1_hi[:, bass.ds(w, F)], start=False, stop=True
                                 ).then_inc(up_done, 1)

            def flip_gelu(i, k):
                t = RING * i + k
                if not real_tile(t):
                    return
                pe.wait_ge(gelu_done, t + 1)
                wait(pe, gelu_t_ready, t - 1)
                for f in range(KF):
                    last = nc.tensor.transpose(flipped[k % 2][:, f * P:(f + 1) * P],
                                               probs[:, k % 2, f * P:(f + 1) * P], ident[:])
                last.then_inc(gelu_flipped, 1)

            def down(i, k, weights):
                t = RING * i + k
                if not real_tile(t):
                    return
                w = weights[k]
                pe.wait_ge(gelu_t_ready, t + 1)
                wait(pe, gated_ready, t - 1)
                for f in range(KF):
                    last = nc.tensor.matmul(mixed[k % 2][:, 0:H], probs_t[:, k % 2, f * P:(f + 1) * P],
                                            w2_sb[:, bass.ds(w + f * H, H)],
                                            start=(f == 0), stop=(f == KF - 1))
                last.then_inc(down_done, 1)

            weights = {}

            def ffn_slot(i, k):
                if not isinstance(i, int) and k == 0:
                    weights.update(load_weights_of(i, -1, RING + 2))
                if isinstance(i, int) and k == -2:
                    weights.update(load_weights_of(0, -1, RING + 4))
                if isinstance(i, int) and k == RING * FFN_TO:
                    weights.update(load_weights_of(0, k - 1, TILES - k + 1))
                flip_rows(i, k + 2)
                up(i, k + 1, weights)
                flip_gelu(i, k)
                down(i, k - 1, weights)

            pe.wait_ge(plan_ready, 1)
            pe.wait_ge(w1_split, E)
            pe.wait_ge(w2_loaded, 16)
            ffn_slots(pe, ffn_slot)

        @block.scalar
        def _(act):
            act.wait_ge(cond_loaded, 16)
            nc.scalar.activation(cond_e[:], cond[:], ACT.Exp, scale=-1.0).then_inc(s_cond_e, 1)
            act.dma_start(wq_sb[:], Wq).then_inc(s_small, 16)
            act.dma_start(bq_sb[:], bq.rearrange("(p a) -> p a", a=1)).then_inc(s_small, 16)
            act.dma_start(wr_sb[:], Wr).then_inc(s_small, 16)
            act.dma_start(br_sb[:], br.rearrange("(a e) -> a e", a=1).to_broadcast([P, E])).then_inc(s_small, 16)

            def normalize1(b):
                if not real(b):
                    return
                act.wait_ge(offset1_ready, b.n + 1)
                act.wait_ge(x_loaded[b.p], 16 * (b.h + 1))
                wait(act, xn_flipped, b.n)
                for j in range(J):
                    last = nc.scalar.activation(xn[:, j, :], x_raw[:, b.p, j, :], ACT.Identity,
                                                bias=offset1[:, b.p, j:j + 1], scale=rstd1[:, b.p, j:j + 1])
                last.then_inc(xn_ready, 1)

            def input_t(b):
                if not real(b):
                    return
                act.wait_ge(xn_flipped, b.n + 1)
                if isinstance(b.n, int) and b.n == 0:
                    act.wait_ge(s_dve0, 6)
                wait(act, q_projected, b.n)
                col = slice(b.n, b.n + 1) if isinstance(b.n, int) else bass.ds(b.n, 1)
                nc.scalar.activation(h_t[:], side[1][:], ACT.Identity, bias=shift1[:, col],
                                     scale=scale1[:, col]).then_inc(h_ready, 1)

            def query(b):
                if not real(b):
                    return
                act.wait_ge(q_projected, b.n + 1)
                if isinstance(b.n, int) and b.n == 0:
                    act.wait_ge(s_small, 64)
                wait(act, q_split, b.n - 1)
                wait(act, v_ready, b.n - 1)
                nc.scalar.activation(q_t[:, b.p, :], side[1][:], ACT.Identity, bias=bq_sb[:, 0:1]
                                     ).then_inc(q_ready, 1)
                nc.scalar.activation(q_hi[:, b.p, :], side[1][:], ACT.Identity, bias=bq_sb[:, 0:1]
                                     ).then_inc(q_hi_ready, 1)

            def exps(b, j):
                if not real(b):
                    return
                act.wait_ge(max_ready, J * b.n + j + 1)
                wait(act, probs_flipped, J * b.n + j - 1)
                wait(act, x1_ready, J * (b.n - 2) + j + 1)
                c = b.p * J + j
                nc.scalar.activation(probs[:, j % 2, :], scores[j % 2][:], ACT.Exp, bias=neg_max[:, c:c + 1],
                                     scale=SCALE, accum_out=den[:, c:c + 1]).then_inc(exp_done, 1)

            def copy_probs(b, j):
                if not real(b):
                    return
                act.wait_ge(probs_flipped, J * b.n + j + 1)
                wait(act, attn_done, J * b.n + j - 1)
                nc.scalar.activation(probs_t[:, j % 2, :], flipped[j % 2][:], ACT.Copy).then_inc(probs_t_ready, 1)

            def router_input(b):
                if not real(b):
                    return
                act.wait_ge(xn2_flipped, b.n + 1)
                wait(act, h2_flipped, b.n)
                col = slice(b.n, b.n + 1) if isinstance(b.n, int) else bass.ds(b.n, 1)
                nc.scalar.activation(h2_t[:], side[0][:], ACT.Identity, bias=shift2[:, col],
                                     scale=scale2[:, col]).then_inc(h2t_ready, 1)

            def copy_x1(b):
                if not real(b):
                    return
                act.wait_ge(x1_ready, J * b.n + J)
                wait(act, scattered[b.p], 16 * J * b.h)
                nc.scalar.activation(payload[:, b.p, :, ROW_X1:ROW_X1 + H], x1[:, b.p, :, :], ACT.Copy
                                     ).then_inc(x1_copied, 1)

            def ffn_input(b):
                if not real(b):
                    return
                act.wait_ge(h2_flipped, b.n + 1)
                wait(act, scattered[b.p], 16 * J * b.h)
                nc.scalar.activation(payload[:, b.p, :, 0:H], side[0][:].rearrange("p (j h) -> p j h", j=J),
                                     ACT.Copy).then_inc(h2_ready, 1)

            def logit_exp(b):
                if not real(b):
                    return
                act.wait_ge(logit_ready, b.n + 1)
                nc.scalar.activation(logit_e[:], logit[:], ACT.Exp, scale=-1.0).then_inc(logit_e_ready, 1)

            def split_w1_hi(e):
                act.wait_ge(w1_loaded, 16)
                at = slice(e * F, (e + 1) * F)
                nc.scalar.activation(w1_hi[:, at], w1_raw[:, at], ACT.Copy).then_inc(w1_half, 1)

            def slot(i, k):
                before2, before, now, after, after2 = (batch_at(i, k + d) for d in range(-2, 3))
                exps(now, 1)
                copy_probs(now, 0)
                query(after)

                exps(now, 2)
                copy_probs(now, 1)
                logit_exp(before2)
                copy_x1(before2)

                exps(now, 3)
                ffn_input(before2)
                copy_probs(now, 2)
                normalize1(after2)

                exps(after, 0)
                copy_probs(now, 3)
                input_t(after2)
                router_input(before)
                for e in W1_SPLITS.get(k, ()) if isinstance(i, int) else ():
                    split_w1_hi(e)

            attention_slots(act, slot)
            act.wait_ge(s_pad0, 2)
            fill_tails(act, mybir.EngineType.Activation, range(E // 2, E))
            nc.scalar.activation(gelu_warm[:], bq_sb[:, 0:1], ACT.Gelu)

            def split_hi(i, k):
                t = RING * i + k
                if not real_tile(t):
                    return
                act.wait_ge(f_flipped, t + 1)
                wait(act, up_done, t - 1)
                nc.scalar.activation(f_hi[:, k % 2, :], side[k % 2][:, 0:P], ACT.Copy).then_inc(f_hi_ready, 1)

            def gelu(i, k):
                t = RING * i + k
                if not real_tile(t):
                    return
                act.wait_ge(up_done, t + 1)
                wait(act, gelu_flipped, t - 1)
                nc.scalar.activation(probs[:, k % 2, :], scores[k % 2][:], ACT.Gelu).then_inc(gelu_done, 1)

            def ffn_slot(i, k):
                split_hi(i, k + 2)
                gelu(i, k + 1)

            ffn_slots(act, ffn_slot)

        @block.vector
        def _(dve):
            def ln1(b):
                if not real(b):
                    return
                wait_apart(dve, x_loaded[b.p], 16 * (b.h + 1))
                for j in range(J):
                    nc.vector.bn_stats(stats1[:, b.p, j, :], x_raw[:, b.p, j, :]).then_inc(ln1_stats, 1)
                for j in range(J):
                    wait_apart(dve, ln1_stats, J * b.n + j + 1)
                    nc.vector.bn_aggr(moments1[:, b.p, j, :], stats1[:, b.p, j, :]).then_inc(ln1_moments, 1)

            def variance1(b):
                if not real(b):
                    return
                dve.wait_ge(ln1_moments, J * b.n + J)
                nc.vector.tensor_scalar_mul(neg_mean1[:, b.p, :], moments1[:, b.p, :, 0], -1.0)
                nc.vector.tensor_scalar_add(var1[:, b.p, :], moments1[:, b.p, :, 1], EPS).then_inc(var1_ready, 1)

            dve.wait_ge(s_cond_e, 1)
            nc.vector.tensor_scalar_add(cond_d[:], cond_e[:], 1.0).then_inc(s_dve0, 1)
            dve.wait_ge(s_dve0, 1)
            nc.vector.reciprocal(cond_s[:], cond_d[:]).then_inc(s_dve0, 1)
            dve.wait_ge(s_dve0, 2)
            nc.vector.tensor_tensor(silu[:], cond[:], cond_s[:], ALU.mult).then_inc(s_silu, 1)
            ln1(batch_at(0, 0))
            variance1(batch_at(0, 0))
            dve.wait_ge(s_silu_tp, 1)
            nc.vector.tensor_copy(silu_t[:], side[0][:, 0:B]).then_inc(s_silu_t, 1)
            ln1(batch_at(0, 1))
            variance1(batch_at(0, 1))
            dve.wait_ge(s_cols, 1)
            nc.vector.tensor_copy(shift1[:], side[1][:, 0:B]).then_inc(s_dve0, 1)
            nc.vector.tensor_scalar_add(scale1[:], side[1][:, B:2 * B], 1.0).then_inc(s_dve0, 1)
            nc.vector.tensor_copy(shift2[:], side[1][:, 2 * B:3 * B]).then_inc(s_dve0, 1)
            nc.vector.tensor_scalar_add(scale2[:], side[1][:, 3 * B:4 * B], 1.0).then_inc(s_dve0, 1)
            dve.wait_ge(s_rowsp, 1)
            g = mixed[1][0:B, 0:2 * H]
            nc.vector.tensor_scalar(gate_sign[:], g, 0.0, 2.0, ALU.is_ge, ALU.mult).then_inc(s_dve0, 1)
            nc.vector.tensor_scalar_mul(gate_neg[:], g, -1.0).then_inc(s_dve0, 1)
            dve.wait_ge(s_dve0, 8)
            nc.vector.scalar_tensor_tensor(gate_size[:], g, 0.25, gate_neg[:], ALU.max, ALU.max).then_inc(s_dve0, 1)
            dve.wait_ge(s_dve0, 9)
            nc.vector.scalar_tensor_tensor(gate_rows[:], gate_sign[:], -1.0, gate_size[:], ALU.add, ALU.mult
                                           ).then_inc(s_mod, 1)
            dve.wait_ge(s_consts, 5)
            nc.vector.tensor_copy(region[:], region_i[:])
            nc.vector.tensor_copy(order[:], order_i[:])
            nc.vector.tensor_copy(tile_no[:], tile_i[:]).then_inc(s_dve0, 1)
            nc.vector.memset(seen[:], 0.0).then_inc(seen_ready, 1)

            def split_q(b):
                if not real(b):
                    return
                dve.wait_ge(q_hi_ready, b.n + 1)
                nc.vector.tensor_sub(q_lo[:, b.p, :], q_t[:, b.p, :], q_hi[:, b.p, :].bitcast(F32)
                                     ).then_inc(q_split, 1)

            def values(b):
                if not real(b):
                    return
                dve.wait_ge(v_flipped, b.n + 1)
                dve.wait_ge(gate1_loaded[b.p], 16 * (b.h + 1))
                nc.vector.tensor_tensor(v_sb[:, b.p, :, :], side[1][:].rearrange("p (j h) -> p j h", j=J),
                                        gate1[:, b.p, :].unsqueeze(1).to_broadcast([P, J, H]), ALU.mult
                                        ).then_inc(v_ready, 1)

            def find_max(b, j):
                if not real(b):
                    return
                dve.wait_ge(scores_ready, J * b.n + j + 1)
                c = b.p * J + j
                nc.vector.tensor_reduce(row_max[:, c:c + 1], scores[j % 2][:], AX_X, ALU.max, negate=True
                                        ).then_inc(max_found, 1)
                dve.wait_ge(max_found, J * b.n + j + 1)
                nc.vector.tensor_scalar_mul(neg_max[:, c:c + 1], row_max[:, c:c + 1], SCALE).then_inc(max_ready, 1)

            def invert_den(b, j):
                if not real(b):
                    return
                dve.wait_ge(exp_done, J * b.n + j + 1)
                c = b.p * J + j
                nc.vector.reciprocal(den_inv[:, c:c + 1], den[:, c:c + 1]).then_inc(den_ready, 1)

            def residual(b, j):
                if not real(b):
                    return
                if j == 0:
                    dve.wait_ge(x_res_loaded[b.p], 16 * (b.h + 1))
                    wait(dve, x1_copied, b.n - 1)
                dve.wait_ge(den_ready, J * b.n + j + 1)
                dve.wait_ge(attn_done, J * b.n + j + 1)
                c = b.p * J + j
                nc.vector.scalar_tensor_tensor(x1[:, b.p, j, :], mixed[j % 2][:, 0:H], den_inv[:, c:c + 1],
                                               x_res[:, b.p, j, :], ALU.mult, ALU.add).then_inc(x1_ready, 1)

            def ln2_stats_of(b, j):
                if not real(b):
                    return
                wait_apart(dve, x1_ready, J * b.n + j + 1)
                nc.vector.bn_stats(stats2[:, b.p, j, :], x1[:, b.p, j, :]).then_inc(ln2_stats, 1)

            def ln2_moments_of(b, j):
                if not real(b):
                    return
                wait_apart(dve, ln2_stats, J * b.n + j + 1)
                nc.vector.bn_aggr(moments2[:, b.p, j, :], stats2[:, b.p, j, :]).then_inc(ln2_moments, 1)
                if j == J - 1:
                    dve.wait_ge(ln2_moments, J * b.n + J)
                    nc.vector.tensor_scalar_add(var2[:, b.p, :], moments2[:, b.p, :, 1], EPS).then_inc(var2_ready, 1)

            def normalize2(b, js):
                if not real(b):
                    return
                dve.wait_ge(rstd2_ready, b.n + 1)
                wait(dve, xn2_flipped, b.n)
                for j in js:
                    last = nc.vector.tensor_scalar(xn2[:, j, :], x1[:, b.p, j, :], moments2[:, b.p, j, 0:1],
                                                   rstd2[:, b.p, j:j + 1], ALU.subtract, ALU.mult)
                if js[-1] == J - 1:
                    last.then_inc(xn2_ready, 1)

            def add_bias(b):
                if not real(b):
                    return
                dve.wait_ge(logits_ready, b.n + 1)
                nc.vector.tensor_tensor(logit[:].rearrange("p (j e) -> p j e", e=E),
                                        side[0][:, 0:J * E].rearrange("p (j e) -> p j e", e=E),
                                        br_sb[:].unsqueeze(1).to_broadcast([P, J, E]), ALU.add
                                        ).then_inc(logit_ready, 1)

            def wide(a):
                return a.unsqueeze(2).to_broadcast([P, J, E])

            def choose(b, part):
                if not real(b):
                    return
                at_expert = logit_d[:].rearrange("p (j e) -> p j e", e=E)
                if part == 0:
                    dve.wait_ge(logit_e_ready, b.n + 1)
                    nc.vector.tensor_scalar_add(logit_d[:], logit_e[:], 1.0).then_inc(route_link, 1)
                else:
                    dve.wait_ge(route_link, 5 * b.n + part)
                if part == 1:
                    nc.vector.tensor_reduce(least_d[:], at_expert, AX_X, ALU.min).then_inc(route_link, 1)
                if part == 2:
                    nc.vector.tensor_tensor(at_max[:], at_expert, wide(least_d[:]), ALU.is_equal
                                            ).then_inc(route_link, 1)
                    wait(dve, gates_ready, b.n)
                    nc.vector.reciprocal(route_max[:], least_d[:]).then_inc(probability_ready, 1)
                if part == 3:
                    nc.vector.tensor_tensor(ranked[:], at_max[:], order[:].unsqueeze(1).to_broadcast([P, J, E]),
                                            ALU.mult).then_inc(route_link, 1)
                if part == 4:
                    nc.vector.tensor_reduce(rank_max[:], ranked[:], AX_X, ALU.max).then_inc(route_link, 1)
                if part == 5:
                    nc.vector.tensor_tensor(mask[:], ranked[:], wide(rank_max[:]), ALU.is_equal
                                            ).then_inc(mask_ready, 1)

            def choose_slots(b, part):
                if not real(b):
                    return
                if part == 0:
                    dve.wait_ge(places_ready, b.n + 1)
                    nc.vector.tensor_tensor(place[:], side[0][:, 0:J * E].rearrange("p (j e) -> p j e", e=E),
                                            region[:, 0:E].unsqueeze(1).to_broadcast([P, J, E]), ALU.add
                                            ).then_inc(place_link, 1)
                    nc.vector.tensor_reduce(batch_count[:], mask[:].rearrange("p j e -> p e j"), AX_X, ALU.add
                                            ).then_inc(place_link, 1)
                if part == 1:
                    dve.wait_ge(place_link, 3 * b.n + 1)
                    nc.vector.tensor_tensor(placed[:], place[:], mask[:], ALU.mult).then_inc(place_link, 1)
                if part == 2:
                    dve.wait_ge(place_link, 3 * b.n + 3)
                    wait(dve, scattered[b.p], 16 * J * b.h)
                    with nc.allow_low_precision("row numbers below 2^24 are exact"):
                        nc.vector.tensor_reduce(slots[:, b.p * J:(b.p + 1) * J], placed[:], AX_X, ALU.add
                                                ).then_inc(slots_ready, 1)
                        nc.vector.tensor_tensor(seen[:], seen[:], batch_count[:], ALU.add).then_inc(seen_ready, 1)

            def slot(i, k):
                before2, before, now, after, after2 = (batch_at(i, k + d) for d in range(-2, 3))
                find_max(now, 1)
                residual(before, 2)
                invert_den(now, 0)
                ln2_stats_of(before, 2)
                if k >= 0:
                    ln1(after2)
                ln2_moments_of(before, 2)
                if k >= 0:
                    variance1(after2)

                find_max(now, 2)
                residual(before, 3)
                add_bias(before2)
                ln2_stats_of(before, 3)
                invert_den(now, 1)
                ln2_moments_of(before, 3)
                split_q(after)
                choose(before2, 0)

                find_max(now, 3)
                choose(before2, 1)
                residual(now, 0)
                choose(before2, 2)
                ln2_stats_of(now, 0)
                choose(before2, 3)
                invert_den(now, 2)
                choose(before2, 4)
                ln2_moments_of(now, 0)
                choose(before2, 5)
                values(after)
                normalize2(before, (0, 1))

                find_max(after, 0)
                normalize2(before, (2, 3))
                choose_slots(before2, 0)
                residual(now, 1)
                invert_den(now, 3)
                ln2_stats_of(now, 1)
                ln2_moments_of(now, 1)
                choose_slots(before2, 1)
                choose_slots(before2, 2)

            attention_slots(dve, slot)

            done = [0]

            def step(ins):
                done[0] += 1
                ins.then_inc(plan_link, 1)
                dve.wait_ge(plan_link, done[0])

            dve.wait_ge(counts_ready, 1)
            step(nc.vector.tensor_copy(counts[:], side[1][:, 0:E]))
            nc.vector.tensor_tensor(tail_row[:], counts[0:1, :], region[0:1, 0:E], ALU.add).then_inc(tails_ready, 1)
            step(nc.vector.tensor_scalar_add(padded_i[:], counts[:], float(P - 1)))
            step(nc.vector.tensor_single_scalar(tiles_i[:], padded_i[:], 7, ALU.arith_shift_right))
            step(nc.vector.tensor_copy(n_tiles[:], tiles_i[:]))
            nc.vector.memset(one_row[:], 1.0)
            step(nc.vector.memset(tiles_to[:, 0:1], 0.0))
            step(nc.vector.tensor_tensor_scan(tiles_to[:, 1:E + 1], one_row[:], n_tiles[:], 0.0,
                                              ALU.mult, ALU.add))
            step(nc.vector.scalar_tensor_tensor(base[:], tiles_to[:], -float(P), region[:], ALU.mult, ALU.add))
            step(nc.vector.tensor_tensor(base_step[:], base[:, 1:E + 1], base[:, 0:E], ALU.subtract))
            step(nc.vector.tensor_tensor(passed[:], tile_no[:].unsqueeze(2).to_broadcast([1, TILES + 1, E]),
                                         tiles_to[0:1, 1:E + 1].unsqueeze(1).to_broadcast([1, TILES + 1, E]),
                                         ALU.is_ge))
            step(nc.vector.tensor_reduce(owner[:], passed[:], AX_X, ALU.add))
            step(nc.vector.tensor_tensor(steps[:], passed[:],
                                         base_step[0:1, :].unsqueeze(1).to_broadcast([1, TILES + 1, E]), ALU.mult))
            step(nc.vector.tensor_reduce(start[:], steps[:], AX_X, ALU.add))
            step(nc.vector.scalar_tensor_tensor(start_f[:], tile_no[:], float(P), start[:], ALU.mult, ALU.add))
            step(nc.vector.tensor_scalar(owner[:], owner[:], float(E - 1), float(F), ALU.min, ALU.mult))
            step(nc.vector.tensor_scalar(tile_row[:], start_f[:], float(E * REGION), None, ALU.min))
            nc.vector.tensor_copy(tile_weights[:], owner[:]).then_inc(plan_ready, 1)

            def split_lo(i, k):
                t = RING * i + k
                if not real_tile(t):
                    return
                dve.wait_ge(f_hi_ready, t + 1)
                nc.vector.tensor_sub(f_lo[:, k % 2, :], side[k % 2][:, 0:P], f_hi[:, k % 2, :].bitcast(F32)
                                     ).then_inc(f_split, 1)

            def copy_gelu(i, k):
                t = RING * i + k
                if not real_tile(t):
                    return
                dve.wait_ge(gelu_flipped, t + 1)
                wait(dve, down_done, t - 1)
                nc.vector.tensor_copy(probs_t[:, k % 2, :], flipped[k % 2][:]).then_inc(gelu_t_ready, 1)

            def finish(i, k):
                t = RING * i + k
                if not real_tile(t):
                    return
                r = k % RING
                dve.wait_ge(down_done, t + 1)
                nc.vector.tensor_tensor(gated[:, k % 2, :], mixed[k % 2][:, 0:H],
                                        rows[:, r, ROW_GATE:ROW_GATE + H], ALU.mult).then_inc(gated_ready, 1)
                dve.wait_ge(gated_ready, t + 1)
                wait(dve, y_scattered[r], 16 * (i + k // RING))
                nc.vector.tensor_copy(tokens[:, r:r + 1], rows[:, r, ROW_ID:ROW_ID + 1].bitcast(I32)
                                      ).then_inc(tokens_kept, 1)
                nc.vector.tensor_tensor(y_out[:, r, :], gated[:, k % 2, :], rows[:, r, ROW_X1:ROW_X1 + H],
                                        ALU.add).then_inc(y_ready, 1)

            def ffn_slot(i, k):
                split_lo(i, k + 2)
                copy_gelu(i, k)
                finish(i, k - 1)

            ffn_slots(dve, ffn_slot)

        @block.gpsimd
        def _(pool):
            nc.gpsimd.memset(ident[:], 0.0).then_inc(s_pool, 1)
            nc.gpsimd.memset(upper[:], 1.0).then_inc(s_pool, 1)
            nc.gpsimd.memset(ones[:], 1.0)
            nc.gpsimd.memset(neg_half[:], -0.5)
            nc.gpsimd.memset(pad_rows[:], 0.0).then_inc(s_pool, 1)
            pool.wait_ge(s_pool, 3)
            nc.gpsimd.affine_select(out=ident[:], in_=ident[:], compare_op=ALU.not_equal, fill=1.0, base=0,
                                    pattern=[[-1, P]], channel_multiplier=1).then_inc(s_consts, 1)
            nc.gpsimd.affine_select(out=upper[:], in_=upper[:], compare_op=ALU.is_gt, fill=0.0, base=0,
                                    pattern=[[1, P]], channel_multiplier=-1).then_inc(s_consts, 1)
            nc.gpsimd.iota(region_i[:], pattern=[[REGION, E + 1]], base=0, channel_multiplier=0).then_inc(s_consts, 1)
            nc.gpsimd.iota(order_i[:], pattern=[[-1, E]], base=E, channel_multiplier=0).then_inc(s_consts, 1)
            nc.gpsimd.iota(tile_i[:], pattern=[[1, TILES + 1]], base=-1, channel_multiplier=0).then_inc(s_consts, 1)
            nc.gpsimd.iota(token_id[:], pattern=[[S, B], [1, J]], base=0, channel_multiplier=J)
            nc.gpsimd.iota(pad_rows[:, ROW_ID:ROW].bitcast(I32), pattern=[[0, ROW - ROW_ID]], base=N,
                           channel_multiplier=0).then_inc(s_pad0, 2)
            nc.gpsimd.memset(payload[:, :, :, ROW_ID:ROW], 0.0).then_inc(s_pool, 1)
            pool.wait_ge(s_pool, 4)

            def invert1(b):
                if not real(b):
                    return
                pool.wait_ge(var1_ready, b.n + 1)
                nc.gpsimd.tensor_tensor(rstd1[:, b.p, :], var1[:, b.p, :], neg_half[:], ALU.pow
                                        ).then_inc(rstd1_ready, 1)
                pool.wait_ge(rstd1_ready, b.n + 1)
                nc.gpsimd.tensor_tensor(offset1[:, b.p, :], neg_mean1[:, b.p, :], rstd1[:, b.p, :], ALU.mult
                                        ).then_inc(offset1_ready, 1)

            def invert2(b):
                if not real(b):
                    return
                pool.wait_ge(var2_ready, b.n + 1)
                nc.gpsimd.tensor_tensor(rstd2[:, b.p, :], var2[:, b.p, :], neg_half[:], ALU.pow
                                        ).then_inc(rstd2_ready, 1)

            def gates(b):
                if not real(b):
                    return
                wait_apart(pool, probability_ready, b.n + 1)
                wait_apart(pool, gate2_loaded[b.p], 16 * (b.h + 1))
                wait_apart(pool, scattered[b.p], 16 * J * b.h)
                for j in range(J):
                    nc.gpsimd.tensor_scalar(payload[:, b.p, j, ROW_GATE:ROW_GATE + H], gate2[:, b.p, :],
                                            route_max[:, j:j + 1], 1.0, ALU.mult, ALU.mult)
                c = slice(b.n * J, (b.n + 1) * J) if isinstance(b.n, int) else bass.ds(b.n * J, J)
                nc.gpsimd.tensor_copy(payload[:, b.p, :, ROW_ID].bitcast(I32), token_id[:, c]
                                      ).then_inc(gates_ready, 1)

            def scatter(b):
                if not real(b):
                    return
                wait_apart(pool, slots_ready, b.n + 1)
                pool.wait_ge(gates_ready, b.n + 1)
                pool.wait_ge(x1_copied, b.n + 1)
                pool.wait_ge(h2_ready, b.n + 1)
                for j in range(J):
                    c = b.p * J + j
                    nc.gpsimd.indirect_dma_start(
                        rows_dram, bass.IndirectOffsetOnAxis(ap=slots[:, c:c + 1], axis=0),
                        payload[:, b.p, j, :], None).then_inc(scattered[b.p], 16)

            def split_w1_lo(e):
                pool.wait_ge(w1_half, e + 1)
                at = slice(e * F, (e + 1) * F)
                nc.gpsimd.tensor_sub(w1_lo[:, at], w1_raw[:, at], w1_hi[:, at].bitcast(F32)
                                     ).then_inc(w1_split, 1)

            def slot(i, k):
                before2, before, after2 = batch_at(i, k - 2), batch_at(i, k - 1), batch_at(i, k + 2)
                invert1(after2)
                invert2(before)
                gates(before2)
                for e in W1_SPLITS.get(k, ()) if isinstance(i, int) else ():
                    split_w1_lo(e)
                scatter(before2)

            attention_slots(pool, slot)

            def write_out(i, k):
                t = RING * i + k
                if not real_tile(t):
                    return
                wait_apart(pool, y_ready, t + 1)
                nc.gpsimd.indirect_dma_start(
                    out_rows, bass.IndirectOffsetOnAxis(ap=tokens[:, k % RING:k % RING + 1], axis=0),
                    y_out[:, k % RING, :], None, bounds_check=N - 1, oob_is_err=False
                ).then_inc(y_scattered[k % RING], 16)

            def ffn_slot(i, k):
                write_out(i, k - 1)

            ffn_slots(pool, ffn_slot)


_INS = ["L0_attn_inputs", "L0_attn_Wq", "L0_attn_bq", "L0_ffn_Wr", "L0_ffn_br", "L0_ffn_W1", "L0_ffn_W2", "L0_c",
        "L0_wmod"]


def kernel(**inputs):
    import numpy as _np
    import concourse.bacc as _bacc
    from concourse import mybir as _mybir
    from concourse.bass_utils import run_bass_kernel_spmd as _run

    nc = _bacc.Bacc("TRN2", target_bir_lowering=False, num_devices=1)
    arrays, args = {}, []
    for name in _INS:
        a = _np.ascontiguousarray(inputs[name])
        arrays[f"in_{name}_dram"] = a
        args.append(nc.dram_tensor(f"in_{name}_dram", a.shape, _mybir.dt.from_np(a.dtype), kind="ExternalInput").ap())
    shape = arrays["in_L0_attn_inputs_dram"].shape
    args.append(nc.dram_tensor("out_0_dram", shape, _mybir.dt.float32, kind="ExternalOutput").ap())
    adaln_block(nc, *args)
    r = _run(nc, [arrays], core_ids=[0])
    return r.results[0]["out_0_dram"]
```
